# Optimizing a Trainium2 kernel written in Bass

```python
import numpy as np
import jax
import jax.numpy as jnp

def _softmax(x, axis=-1):
    return jax.nn.softmax(x, axis=axis)

def _gelu(x):
    return jax.nn.gelu(x, approximate=True)

def _silu(x):
    return jax.nn.silu(x)

def _sigmoid(x):
    return jax.nn.sigmoid(x)

def _layernorm(x, axis=-1, eps=1e-05):
    m = jnp.mean(x, axis=axis, keepdims=True)
    v = jnp.var(x, axis=axis, keepdims=True)
    return (x - m) / jnp.sqrt(v + eps)

def _scatter_add(tgt, idx, src, axis=0):
    return tgt.at[idx].add(src)

def _segment_sum(src, seg, n):
    return jax.ops.segment_sum(src, seg, n)
kernel_name = 'mk_adj_resnorm_d1_adj_r2_12a254'

def setup_inputs(seed: int=0):
    np.random.seed(seed)
    _w = jnp.asarray

    def _rec_inputs():
        import jax
        import jax.numpy as jnp
        _gk = jax.random.key(seed)
        x = 7.22e-05 + 1 * jax.random.normal(jax.random.fold_in(_gk, 1), (4096, 512), jnp.float32)
        _a = jax.random.bernoulli(jax.random.fold_in(_gk, 2), 0.00195312, (4096, 4096))
        _a = jnp.logical_or(_a, jnp.swapaxes(_a, -1, -2))
        _a = jnp.logical_or(_a, jnp.eye(4096, dtype=bool))
        _af = _a.astype(jnp.float32)
        adj = _af
        return (x, adj)
    x, adj = _rec_inputs()

    def _L0_gnn_setup():
        import jax, jax.numpy as jnp
        import numpy as np
        N = 4096
        D = 512
        key = jax.random.key(seed)
        ks = jax.random.split(key, 13)
        w_scale = 1.0 / np.sqrt(D)
        inp = {'query': jax.random.normal(ks[0], (N, D), dtype=jnp.float32), 'key': jax.random.normal(ks[1], (N, D), dtype=jnp.float32), 'value': jax.random.normal(ks[2], (N, D), dtype=jnp.float32), 'adj_matrix': jax.random.randint(ks[3], (N, N), 0, 2).astype(jnp.float32), 'Wq': jax.random.normal(ks[4], (D, D), dtype=jnp.float32) * w_scale, 'bq': jax.random.normal(ks[5], (D,), dtype=jnp.float32) * 0.01, 'Wk': jax.random.normal(ks[6], (D, D), dtype=jnp.float32) * w_scale, 'bk': jax.random.normal(ks[7], (D,), dtype=jnp.float32) * 0.01, 'Wv': jax.random.normal(ks[8], (D, D), dtype=jnp.float32) * w_scale, 'bv': jax.random.normal(ks[9], (D,), dtype=jnp.float32) * 0.01, 'Wm': jax.random.normal(ks[10], (D, D), dtype=jnp.float32) * w_scale, 'bm': jax.random.normal(ks[11], (D,), dtype=jnp.float32) * 0.01}
        return inp
    _L0_gnn_all = _L0_gnn_setup()
    _L0_gnn_in = {k: v for k, v in _L0_gnn_all.items() if k in ('key', 'value', 'Wq', 'bq', 'Wk', 'bk', 'Wv', 'bv', 'Wm', 'bm')}
    del _L0_gnn_all
    return {'x': x, 'adj': adj, 'L0_gnn_key': _L0_gnn_in['key'], 'L0_gnn_value': _L0_gnn_in['value'], 'L0_gnn_Wq': _L0_gnn_in['Wq'], 'L0_gnn_bq': _L0_gnn_in['bq'], 'L0_gnn_Wk': _L0_gnn_in['Wk'], 'L0_gnn_bk': _L0_gnn_in['bk'], 'L0_gnn_Wv': _L0_gnn_in['Wv'], 'L0_gnn_bv': _L0_gnn_in['bv'], 'L0_gnn_Wm': _L0_gnn_in['Wm'], 'L0_gnn_bm': _L0_gnn_in['bm']}

def reference(x, adj, L0_gnn_key, L0_gnn_value, L0_gnn_Wq, L0_gnn_bq, L0_gnn_Wk, L0_gnn_bk, L0_gnn_Wv, L0_gnn_bv, L0_gnn_Wm, L0_gnn_bm):
    import jax
    import jax.numpy as jnp

    def _L0_gnn_ref(query, key, value, adj_matrix, Wq, bq, Wk, bk, Wv, bv, Wm, bm):
        import jax, jax.numpy as jnp
        import numpy as np
        N = 4096
        D = 512
        q = query @ Wq.T + bq
        k = key @ Wk.T + bk
        v = value @ Wv.T + bv
        scale = q.shape[0] ** 0.5
        scores = jnp.einsum('nd,md->nm', q, k) / scale
        adj_scores = scores * adj_matrix
        adj_scores = jnp.where(jnp.abs(adj_scores) < 1e-05, -1000000000.0, adj_scores)
        prob = jax.nn.softmax(adj_scores, axis=-1)
        x = jnp.einsum('nm,md->nd', prob, v)
        return x @ Wm.T + bm
    x = _layernorm(x + _L0_gnn_ref(x, L0_gnn_key, L0_gnn_value, adj, L0_gnn_Wq, L0_gnn_bq, L0_gnn_Wk, L0_gnn_bk, L0_gnn_Wv, L0_gnn_bv, L0_gnn_Wm, L0_gnn_bm), axis=-1)
    return x

_drawn_inputs = setup_inputs


def setup_inputs(seed=0):
    import zlib

    import numpy as np

    out = dict(_drawn_inputs(seed))
    spreads = {}
    factors = {'L0_gnn_bq': 64.0, 'L0_gnn_bk': 64.0, 'L0_gnn_bv': 6.107, 'L0_gnn_bm': 5.687}
    for name, (base, spread) in spreads.items():
        noise = np.random.default_rng([zlib.crc32(name.encode()), seed]).standard_normal(out[name].shape)
        drawn = base * np.exp(spread * noise) if base else spread * noise
        out[name] = jnp.asarray(drawn.astype(out[name].dtype))
    for name, factor in factors.items():
        out[name] = (out[name] * factor).astype(out[name].dtype)
    return out
```

```python
from contextlib import ExitStack

import concourse.bass as bass
from concourse import mybir

ALU = mybir.AluOpType
ACT = mybir.ActivationFunctionType
AX = mybir.AxisListType
F32 = mybir.dt.float32
F32R = mybir.dt.float32r
BF16 = mybir.dt.bfloat16
I32 = mybir.dt.int32

P = 128
N = 4096
D = 512
C = D // P
W = 512
G = W // P
NB = N // W
SCALE = 1.0 / float(N) ** 0.5
CUT = 1e-5
MASKED = -1e9
EPS = 1e-5
LN_OPS = 2 + 4 * 3 + 1


def gnn_attention_kernel(nc, x, adj, xT, keyT, valT, Wq, Wk, Wv, WmT, bq, bk, bv, bm, ident_in,
                         q_scratch, out):
    adj_t = adj.rearrange("(b g p) (j m) -> b j g p m", g=G, p=P, m=W)
    x_t = x.rearrange("(b g p) d -> b p g d", g=G, p=P)
    out_t = out.rearrange("(b g p) d -> b p g d", g=G, p=P)

    with ExitStack() as ctx:
        def sb(name, shape, dt=F32, where=ctx):
            return where.enter_context(nc.sbuf_tensor(name, [P] + shape, dt))

        def sem(name):
            return ctx.enter_context(nc.semaphore(name))

        acc = ctx.enter_context(nc.psum_tensor("acc", [P, G, W], F32))
        ps_s = ctx.enter_context(nc.psum_tensor("ps_s", [P, 2, W], F32))
        ps_t = ctx.enter_context(nc.psum_tensor("ps_t", [P, 2, W], F32))

        ident = sb("ident", [P])
        ones = sb("ones", [P])
        bq_c, bk_c, bv_c = sb("bq_c", [C]), sb("bk_c", [C]), sb("bv_c", [C])
        qbias = sb("qbias", [C])
        rbias = sb("rbias", [1])
        r_new = sb("r_new", [G])
        r_all = sb("r_all", [NB * G])
        mx, mx_tile, neg_mx = sb("mx", [G]), sb("mx_tile", [G]), sb("neg_mx", [G])
        esum, rowsum, rinv = sb("esum", [G]), sb("rowsum", [G]), sb("rinv", [G])
        stats, mv = sb("stats", [G, 6]), sb("mv", [G, 2])
        ve, rs, nt = sb("ve", [G]), sb("rs", [G]), sb("nt", [G])
        raw = [sb("raw0", [C, W])]
        hi = [sb("hi0", [C, W], F32R)]
        lo = [sb("lo0", [C, W], F32R)]
        q_hl = sb("q_hl", [C, 2, W], F32R)
        adj_s = sb("adj_s", [G, W])
        mag = sb("mag", [2, W])
        cut = sb("cut", [W], BF16)
        y = sb("y", [G, W])

        with ExitStack() as early:
            wvm_h, wvm_l = (sb(n, [C, D], F32R, early) for n in ("wvm_h", "wvm_l"))
            vbias = sb("vbias", [D], F32, early)
            w1 = sb("w1", [D], F32, early)
            m_h, m_l = (sb(n, [C, D], F32R, early) for n in ("m_h", "m_l"))
            q_out = sb("q_out", [C, 2, W], F32R, early)
            sb("pad_a", [12 * 256 + 0], F32, early)
            wq_s, wk_s, wv_s, wm_s = (sb(n, [C, D], F32, early) for n in ("wq_s", "wk_s", "wv_s", "wm_s"))
            bk_r, bv_r = sb("bk_r", [C, P], F32, early), sb("bv_r", [C, P], F32, early)
            bm_r = sb("bm_r", [D], F32, early)
        t_s = sb("t_s", [G, NB, W])
        v_s = sb("v_s", [NB * G, D])

        with ExitStack() as stream:
            raw.append(sb("raw1", [C, W], F32, stream))
            hi.append(sb("hi1", [C, W], F32R, stream))
            lo.append(sb("lo1", [C, W], F32R, stream))
        prob = sb("prob", [G, W])
        p_h, p_l = sb("p_h", [2, W], F32R), sb("p_l", [2, W], F32R)
        v_h, v_l = sb("v_h", [2, D], F32R), sb("v_l", [2, D], F32R)

        wqk_in, wvm_in = sem("wqk_in"), sem("wvm_in")
        raw_in = [sem("raw_in0"), sem("raw_in1")]
        y_in = sem("y_in")
        q_in = sem("q_in")
        adj_in = [sem(f"adj_in{g}") for g in range(G)]
        q_stored = [sem(f"q_stored{c}") for c in range(C)]
        out_stored = sem("out_stored")
        reps = sem("reps")
        wmm = sem("wmm")
        w_hi = sem("w_hi")
        hi_done, lo_done = sem("hi_done"), sem("lo_done")
        group = sem("group")
        acc_free = sem("acc_free")
        q_hi = sem("q_hi")
        r_part, r_done = sem("r_part"), sem("r_done")
        s_read = sem("s_read")
        mag_done = sem("mag_done")
        cut_done, t_done = sem("cut_done"), sem("t_done")
        mx_part, mx_done = sem("mx_part"), sem("mx_done")
        exp_done = sem("exp_done")
        sum_done = sem("sum_done")
        turned = sem("turned")
        ph_done, pl_done = sem("ph_done"), sem("pl_done")
        vh_done, vl_done = sem("vh_done"), sem("vl_done")
        pv_done = sem("pv_done")
        rinv_done = sem("rinv_done")
        acc_read = sem("acc_read")
        aggr_done = sem("aggr_done")
        ln_op = sem("ln_op")
        ln_done = sem("ln_done")

        KEY0 = 2 * NB
        STREAM = KEY0 + NB
        block = ctx.enter_context(nc.Block())

        @block.sync
        def _(sp):
            for dst, src in ((wq_s, Wq), (wk_s, Wk)):
                sp.dma_start(dst[:], src.rearrange("(c p) d -> p c d", p=P)).then_inc(wqk_in, 16)
            for dst, src in ((bq_c, bq), (bk_c, bk)):
                sp.dma_start(dst[:], src).then_inc(wqk_in, 16)
            sp.dma_start(raw[0][:], xT[0]).then_inc(raw_in[0], 16)
            for dst, src in ((wv_s, Wv), (wm_s, WmT)):
                sp.dma_start(dst[:], src.rearrange("(c p) d -> p c d", p=P)).then_inc(wvm_in, 16)
            for dst, src in ((bv_c[:], bv), (bm_r[0:1, :], bm), (ident[:], ident_in)):
                sp.dma_start(dst, src).then_inc(wvm_in, 16)
            sp.dma_start(raw[1][:], xT[1]).then_inc(raw_in[1], 16)
            sp.dma_start(y[:], x_t[0]).then_inc(y_in, 16)

            def load_raw(k, tile, number):
                sp.wait_ge(lo_done, number - 1)
                sp.dma_start(raw[k][:], tile).then_inc(raw_in[k], 16)

            def store_q(b):
                for c in range(C):
                    sp.wait_ge(acc_free, 2 * C + 4 * b + c + 1)
                    sp.dma_start(q_scratch[b, :, c], q_out[:, c].bitcast(F32)).then_inc(q_stored[c], 16)

            def x_rows(b):
                sp.wait_ge(r_done, b + 1)
                sp.dma_start(y[:], x_t[b + 1]).then_inc(y_in, 16)

            with sp.Fori(0, NB // 2 - 1) as pair:
                for k in range(2):
                    load_raw(k, xT[2 * pair + k + 2], 2 * pair + k + 2)
                    x_rows(2 * pair + k)
                    store_q(2 * pair + k)
            load_raw(0, valT[0], NB)
            x_rows(NB - 2)
            store_q(NB - 2)
            load_raw(1, valT[1], NB + 1)
            store_q(NB - 1)
            sp.wait_ge(r_done, NB)
            sp.dma_start(y[:], x_t[0]).then_inc(y_in, 16)
            for c in range(C):
                sp.wait_ge(q_stored[c], 16 * NB)
            sp.dma_start(q_hl[:].bitcast(F32), q_scratch[0]).then_inc(q_in, 16)
            for g in range(G):
                sp.dma_start(adj_s[:, g], adj_t[0, 0, g]).then_inc(adj_in[g], 16)
            with sp.Fori(1, NB // 2) as pair:
                for k in range(2):
                    load_raw(k, valT[2 * pair + k], 2 * pair + k + NB)
            for k in range(2):
                load_raw(k, keyT[k], KEY0 + k)

            def load_adj(b, j, t, groups=range(G)):
                for g in groups:
                    sp.wait_ge(t_done, 4 * t + g - 3)
                    sp.dma_start(adj_s[:, g], adj_t[b, j, g]).then_inc(adj_in[g], 16)

            def load_key(j, t):
                sp.wait_ge(lo_done, KEY0 + t)
                sp.dma_start(raw[0][:], keyT[j]).then_inc(raw_in[0], 16)

            load_adj(0, 1, 1)
            with sp.Fori(1, NB // 2) as pair:
                for k in range(2):
                    load_raw(k, keyT[2 * pair + k], 2 * pair + k + KEY0)
                    load_adj(0, 2 * pair + k, 2 * pair + k)
            load_raw(0, keyT[0], STREAM)

            def open_block(b):
                load_adj(b, 0, NB * b, range(3))
                sp.wait_ge(group, 4 * KEY0 + 4 * NB * b)
                sp.dma_start(q_hl[:].bitcast(F32), q_scratch[b]).then_inc(q_in, 16)
                load_adj(b, 0, NB * b, range(3, G))
                load_key(1, NB * b + 1)
                load_adj(b, 1, NB * b + 1)

            def turn_y(b):
                sp.wait_ge(ln_done, 4 * b + 4)
                sp.dma_start(out_t[b], y[:]).then_inc(out_stored, 16)
                sp.wait_ge(out_stored, 16 * b + 16)

            def rest(b):
                with sp.Fori(2, NB) as j:
                    t = sp.snap(NB * b + j)
                    load_key(j, t)
                    load_adj(b, j, t)

            open_block(1)
            rest(1)
            with sp.Fori(2, NB) as b:
                load_key(0, NB * b)
                open_block(b)
                turn_y(b - 2)
                sp.dma_start(y[:], x_t[b - 1]).then_inc(y_in, 16)
                rest(b)
            turn_y(NB - 2)
            sp.dma_start(y[:], x_t[NB - 1]).then_inc(y_in, 16)
            turn_y(NB - 1)

        @block.tensor
        def _(pe):
            def times(out, a, b, start, stop, last=True):
                n = len(a)
                for i, ((ah, al), (bh, bl)) in enumerate(zip(a, b)):
                    pe.matmul(out, ah, bh, start=start and i == 0, stop=False, skip_group_check=True)
                    pe.matmul(out, ah, bl, start=False, stop=False, skip_group_check=True)
                    mm = pe.matmul(out, al, bh, start=False, stop=stop and i == n - 1, skip_group_check=True)
                return mm

            pe.wait_ge(wqk_in, 64)
            for c in range(C):
                for o in range(C):
                    mm = pe.matmul(acc[:, c], wq_s[:, o, c * P:(c + 1) * P], wk_s[:, o], start=o == 0, stop=o == C - 1)
                mm.then_inc(wmm, 1)
            pe.wait_ge(wvm_in, 80)
            for c in range(C):
                bank = (ps_s if c < 2 else ps_t)[:, c % 2]
                for o in range(C):
                    mm = pe.matmul(bank, wv_s[:, o, c * P:(c + 1) * P], wm_s[:, o], start=o == 0, stop=o == C - 1)
                mm.then_inc(wmm, 1)
            pe.wait_ge(reps, 2)
            pe.wait_ge(acc_free, 1)
            for o in range(C):
                mm = pe.matmul(acc[:, 0], bk_r[:, o], wq_s[:, o], start=o == 0, stop=o == C - 1)
            mm.then_inc(wmm, 1)
            pe.wait_ge(acc_free, 2)
            for o in range(C):
                pe.matmul(acc[:, 1], bv_r[:, o], wm_s[:, o], start=o == 0, stop=False)
            pe.matmul(acc[:, 1], ones[0:1, :], bm_r[0:1, :], start=False, stop=True).then_inc(wmm, 1)
            pe.wait_ge(acc_free, 3)
            for c in range(C):
                for o in range(C):
                    mm = pe.matmul(acc[:, 2, c:c + 1], wk_s[:, o, c * P:(c + 1) * P], bq_c[:, o:o + 1],
                                   start=o == 0, stop=o == C - 1)
            mm.then_inc(wmm, 1)
            pe.wait_ge(acc_free, 4)
            for o in range(C):
                mm = pe.matmul(acc[:, 3, 0:1], bk_r[:, o], bq_c[:, o:o + 1], start=o == 0, stop=o == C - 1)
            mm.then_inc(wmm, 1)

            def project_x(k, b):
                pe.wait_ge(lo_done, b + 1)
                for e in range(C):
                    pe.wait_ge(acc_free, 4 * b + e + 5)
                    cols = slice(e * P, (e + 1) * P)
                    times(acc[:, e], [(m_h[:, c, cols], m_l[:, c, cols]) for c in range(C)],
                          [(hi[k][:, c], lo[k][:, c]) for c in range(C)], True, True).then_inc(group, 1)

            with pe.Fori(0, NB // 2) as pair:
                for k in range(2):
                    project_x(k, 2 * pair + k)

            def project_value(k, j):
                pe.wait_ge(lo_done, NB + j + 1)
                for e in range(G):
                    pe.wait_ge(acc_free, 4 * NB + 4 * j + e + 5)
                    cols = slice(e * P, (e + 1) * P)
                    times(acc[:, e], [(hi[k][:, c, cols], lo[k][:, c, cols]) for c in range(C)],
                          [(wvm_h[:, c], wvm_l[:, c]) for c in range(C)], True, True).then_inc(group, 1)

            with pe.Fori(0, NB // 2) as pair:
                for k in range(2):
                    project_value(k, 2 * pair + k)

            def scores(k, t, g):
                if g == 0:
                    pe.wait_ge(lo_done, KEY0 + 1 + t)
                pe.wait_ge(s_read, 4 * t + g + 1)
                rows = slice(g * P, (g + 1) * P)
                times(ps_s[:, g % 2], [(q_hl[:, c, 0, rows], q_hl[:, c, 1, rows]) for c in range(C)],
                      [(hi[k][:, c], lo[k][:, c]) for c in range(C)], True, True).then_inc(group, 1)

            def turn(u, c):
                if c == 0:
                    pe.wait_ge(exp_done, 4 * u + 4)
                for g in range(G):
                    mm = pe.transpose(ps_t[:, c % 2, g * P:(g + 1) * P], prob[:, g, c * P:(c + 1) * P], ident[:])
                mm.then_inc(turned, 1)

            def product(u, c, first):
                pe.wait_ge(pl_done, 4 * u + c + 1)
                pe.wait_ge(vl_done, 4 * u + c + 1)
                for g in range(G):
                    rows = slice(g * P, (g + 1) * P)
                    mm = times(acc[:, g], [(p_h[:, c % 2, rows], p_l[:, c % 2, rows])],
                               [(v_h[:, c % 2], v_l[:, c % 2])], first and c == 0, False)
                mm.then_inc(pv_done, 1)

            def step(u, first=False, with_scores=True):
                if with_scores:
                    for g in range(3):
                        scores(0, u + NB, g)
                turn(u, 0)
                if with_scores:
                    scores(0, u + NB, 3)
                turn(u, 1)
                if first:
                    pe.wait_ge(acc_read, first[0])
                for c in range(4):
                    product(u, c, bool(first))
                    if c < 2:
                        turn(u, c + 2)

            pe.wait_ge(q_in, 16)
            with pe.Fori(0, NB // 2) as pair:
                for k in range(2):
                    for g in range(G):
                        scores(k, 2 * pair + k, g)
            pe.wait_ge(q_in, 32)
            step(0, first=(0,))
            with pe.Fori(0, NB - 2) as b:
                with pe.Fori(1, NB) as j:
                    step(pe.snap(NB * b + j))
                pe.wait_ge(q_in, 16 * b + 48)
                step(pe.snap(NB * b + NB), first=(4 * b + 4,))
            with pe.Fori(1, NB) as j:
                step(pe.snap(NB * (NB - 2) + j))
            step(NB * (NB - 1), first=(4 * (NB - 1),), with_scores=False)
            with pe.Fori(1, NB) as j:
                step(pe.snap(NB * (NB - 1) + j), with_scores=False)

        @block.scalar
        def _(act):
            def split_hi(k, number, loads, groups, pieces=range(1)):
                act.wait_ge(raw_in[k], 16 * loads)
                if groups is not None:
                    act.wait_ge(group, groups)
                act.activation(hi[k][:], raw[k][:], ACT.Copy).then_inc(hi_done, 1)

            split_hi(0, 0, 1, None)
            for c in range(C):
                act.wait_ge(wmm, c + 1)
                act.activation(m_h[:, c], acc[:, c], ACT.Copy, scale=SCALE).then_inc(w_hi, 1)
            for c in range(C):
                act.wait_ge(wmm, C + c + 1)
                act.activation(wvm_h[:, c], (ps_s if c < 2 else ps_t)[:, c % 2], ACT.Copy).then_inc(w_hi, 1)

            def q_parts(b):
                for c in range(C):
                    act.wait_ge(group, 4 * b + c + 1)
                    if not (isinstance(b, int) and b == 0):
                        act.wait_ge(q_stored[c], 16 * b)
                    act.activation(q_out[:, c, 0], acc[:, c], ACT.Identity, bias=qbias[:, c:c + 1]).then_inc(q_hi, 1)

            act.wait_ge(acc_free, 2 * C)
            split_hi(1, 1, 1, None)
            q_parts(0)
            split_hi(0, 2, 2, 4)
            q_parts(1)
            with act.Fori(1, NB // 2) as pair:
                for k in range(2):
                    b = 2 * pair + k
                    split_hi(1 - k, b + 1, pair + 1 + k, 4 * b)
                    q_parts(b)
            with act.Fori(NB // 2, KEY0 // 2) as pair:
                for k in range(2):
                    split_hi(1 - k, 2 * pair + k + 1, pair + 1 + k, 8 * pair + 4 * k)

            def magnitude(t, g):
                act.wait_ge(s_read, 4 * t + g + 3)
                act.activation(mag[:, g % 2], adj_s[:, g], ACT.Abs).then_inc(mag_done, 1)

            def exps(u, b, j):
                act.wait_ge(mx_done, b + 1)
                act.wait_ge(turned, 4 * u)
                act.wait_ge(sum_done, u)
                for g in range(G):
                    act.activation(prob[:, g], t_s[:, g, j], ACT.Exp, bias=neg_mx[:, g:g + 1],
                                   accum_out=esum[:, g:g + 1]).then_inc(exp_done, 1)

            def parts(u, j, c):
                act.wait_ge(turned, 4 * u + c + 1)
                act.activation(p_h[:, c % 2], ps_t[:, c % 2], ACT.Copy).then_inc(ph_done, 1)
                act.activation(v_h[:, c % 2], v_s[:, 4 * j + c], ACT.Copy).then_inc(vh_done, 1)

            with act.Fori(KEY0 // 2, STREAM // 2) as pair:
                for k in range(2):
                    split_hi(1 - k, 2 * pair + k + 1, pair + 1 + k, 8 * pair + 4 * k)
                    for g in range(G):
                        magnitude(2 * pair + k - KEY0, g)

            def step(u, b, j, with_scores=True, ahead=True):
                exps(u, b, j)
                if with_scores:
                    for g in range(3):
                        magnitude(u + NB, g)
                for c in range(4):
                    parts(u, j, c)
                    if c == 1 and with_scores:
                        magnitude(u + NB, 3)
                    if c == 1 and ahead:
                        split_hi(0, KEY0 + NB + u + 1, 6 + NB + u, 4 * KEY0 + 4 * NB + 4 + 4 * u)

            step(0, 0, 0)
            with act.Fori(0, NB - 2) as b:
                with act.Fori(1, NB) as j:
                    step(act.snap(NB * b + j), b, j)
                step(act.snap(NB * b + NB), b + 1, 0)
            with act.Fori(1, NB - 1) as j:
                step(act.snap(NB * (NB - 2) + j), NB - 2, j)
            step(NB * (NB - 1) - 1, NB - 2, NB - 1, ahead=False)
            with act.Fori(0, NB) as j:
                step(act.snap(NB * (NB - 1) + j), NB - 1, j, with_scores=False, ahead=False)

        @block.vector
        def _(dve):
            def minus_hi(lo_part, whole, hi_part):
                return dve.tensor_tensor(lo_part, whole, hi_part.bitcast(F32), ALU.subtract)

            def split_lo(k, number):
                dve.wait_ge(hi_done, number + 1)
                minus_hi(lo[k][:], raw[k][:], hi[k][:]).then_inc(lo_done, 1)

            dve.memset(ones[:], 1.0).then_inc(reps, 1)
            dve.wait_ge(wqk_in, 64)
            dve.wait_ge(wvm_in, 80)
            dve.wait_ge(reps, 1)
            for o in range(C):
                dve.tensor_scalar(bk_r[:, o], ones[:], bk_c[:, o:o + 1], None, ALU.mult)
                last = dve.tensor_scalar(bv_r[:, o], ones[:], bv_c[:, o:o + 1], None, ALU.mult)
            last.then_inc(reps, 1)
            split_lo(0, 0)
            for c in range(C):
                dve.wait_ge(w_hi, c + 1)
                dve.scalar_tensor_tensor(m_l[:, c], acc[:, c], SCALE, m_h[:, c].bitcast(F32),
                                         ALU.mult, ALU.subtract).then_inc(acc_free, 1)
            for c in range(C):
                dve.wait_ge(w_hi, C + c + 1)
                low = minus_hi(wvm_l[:, c], (ps_s if c < 2 else ps_t)[:, c % 2], wvm_h[:, c])
                if c < 2:
                    low.then_inc(s_read, 1)
            dve.wait_ge(wmm, 2 * C + 1)
            dve.tensor_scalar(w1[:], acc[:, 0], SCALE, None, ALU.mult).then_inc(acc_free, 1)
            dve.wait_ge(wmm, 2 * C + 2)
            dve.tensor_copy(vbias[:], acc[:, 1]).then_inc(acc_free, 1)
            dve.wait_ge(wmm, 2 * C + 3)
            dve.tensor_scalar(qbias[:], acc[:, 2, 0:C], SCALE, None, ALU.mult).then_inc(acc_free, 1)
            dve.wait_ge(wmm, 2 * C + 4)
            dve.tensor_scalar(rbias[:], acc[:, 3, 0:1], SCALE, None, ALU.mult).then_inc(acc_free, 1)
            dve.wait_ge(acc_free, 2 * C)

            with dve.Fori(0, NB // 2) as pair:
                for k in range(2):
                    b = 2 * pair + k
                    split_lo(1 - k, b + 1)
                    dve.wait_ge(y_in, 16 * b + 16)
                    for g in range(G):
                        dve.tensor_tensor_reduce(y[:, g], y[:, g], w1[:], 1.0, 0.0, ALU.mult, ALU.add,
                                                 r_new[:, g:g + 1]).then_inc(r_part, 1)
                    dve.wait_ge(r_part, 4 * b + 4)
                    dve.tensor_scalar(r_all[:, bass.ds(4 * b, G)], r_new[:], rbias[:, 0:1], None,
                                      ALU.add).then_inc(r_done, 1)
                    for c in range(C):
                        dve.wait_ge(q_hi, 4 * b + c + 1)
                        dve.scalar_tensor_tensor(q_out[:, c, 1], acc[:, c], qbias[:, c:c + 1],
                                                 q_out[:, c, 0].bitcast(F32), ALU.add,
                                                 ALU.subtract).then_inc(acc_free, 1)

            with dve.Fori(0, NB // 2) as pair:
                for k in range(2):
                    j = 2 * pair + k
                    split_lo(1 - k, NB + j + 1)
                    for c in range(G):
                        dve.wait_ge(group, 4 * NB + 4 * j + c + 1)
                        dve.tensor_tensor(v_s[:, 4 * j + c], acc[:, c], vbias[:], ALU.add).then_inc(acc_free, 1)

            def masked(b, j, t, g):
                dve.wait_ge(group, 4 * KEY0 + 4 * t + g + 1)
                dve.wait_ge(adj_in[g], 16 * t + 16)
                dve.scalar_tensor_tensor(adj_s[:, g], ps_s[:, g % 2], r_all[:, bass.ds(4 * b + g, 1)],
                                         adj_s[:, g], ALU.add, ALU.mult).then_inc(s_read, 1)
                dve.wait_ge(mag_done, 4 * t + g + 1)
                dve.tensor_scalar(cut[:], mag[:, g % 2], CUT, None, ALU.is_lt).then_inc(cut_done, 1)
                dve.wait_ge(cut_done, 4 * t + g + 1)
                dve.scalar_tensor_tensor(t_s[:, g, j], cut[:], MASKED, adj_s[:, g],
                                         ALU.mult, ALU.add).then_inc(t_done, 1)

            def maximum(j, t, first):
                dve.drain()
                if first:
                    dve.tensor_reduce(mx[:], t_s[:, :, j], AX.X, ALU.max).then_inc(mx_part, 2)
                else:
                    dve.tensor_reduce(mx_tile[:], t_s[:, :, j], AX.X, ALU.max).then_inc(mx_part, 1)
                    dve.wait_ge(mx_part, 2 * t + 1)
                    dve.tensor_tensor(mx[:], mx[:], mx_tile[:], ALU.max).then_inc(mx_part, 1)

            def block_maximum(b):
                dve.wait_ge(mx_part, 2 * NB * (b + 1))
                dve.tensor_scalar(neg_mx[:], mx[:], -1.0, None, ALU.mult).then_inc(mx_done, 1)

            def parts(u, j, c):
                dve.wait_ge(ph_done, 4 * u + c + 1)
                minus_hi(p_l[:, c % 2], ps_t[:, c % 2], p_h[:, c % 2]).then_inc(pl_done, 1)
                dve.wait_ge(vh_done, 4 * u + c + 1)
                minus_hi(v_l[:, c % 2], v_s[:, 4 * j + c], v_h[:, c % 2]).then_inc(vl_done, 1)

            def sums(u, first):
                dve.wait_ge(exp_done, 4 * u + 4)
                if first:
                    dve.tensor_copy(rowsum[:], esum[:]).then_inc(sum_done, 1)
                else:
                    dve.wait_ge(sum_done, u)
                    dve.tensor_tensor(rowsum[:], rowsum[:], esum[:], ALU.add).then_inc(sum_done, 1)

            def take_out(b):
                dve.wait_ge(sum_done, NB * b + NB)
                dve.reciprocal(rinv[:], rowsum[:]).then_inc(rinv_done, 1)
                dve.wait_ge(rinv_done, b + 1)
                dve.wait_ge(pv_done, 4 * NB * b + 4 * NB)
                dve.wait_ge(y_in, 16 * (NB + b + 1))
                for g in range(G):
                    dve.scalar_tensor_tensor(y[:, g], acc[:, g], rinv[:, g:g + 1], y[:, g],
                                             ALU.mult, ALU.add).then_inc(acc_read, 1)

            def ln_stats(b, g):
                dve.wait_ge(acc_read, 4 * b + g + 1)
                dve.bn_stats(stats[:, g], y[:, g])

            def ln_scale(b):
                dve.drain()
                for g in range(G):
                    dve.bn_aggr(mv[:, g], stats[:, g]).then_inc(aggr_done, 1)
                dve.wait_ge(aggr_done, 4 * b + 4)
                count = [0]

                def link(instruction):
                    count[0] += 1
                    instruction.then_inc(ln_op, 1)
                    dve.wait_ge(ln_op, LN_OPS * b + count[0])

                link(dve.tensor_scalar(ve[:], mv[:, :, 1], EPS, None, ALU.add))
                link(dve.tensor_scalar(nt[:].bitcast(I32), ve[:].bitcast(I32), 1, None, ALU.arith_shift_right))
                link(dve.tensor_scalar(rs[:].bitcast(I32), nt[:].bitcast(I32), -1.0, float(0x5f3759df), ALU.mult, ALU.add))
                for _ in range(3):
                    link(dve.tensor_tensor(nt[:], rs[:], rs[:], ALU.mult))
                    link(dve.tensor_tensor(nt[:], nt[:], ve[:], ALU.mult))
                    link(dve.tensor_scalar(nt[:], nt[:], -0.5, 1.5, ALU.mult, ALU.add))
                    link(dve.tensor_tensor(rs[:], rs[:], nt[:], ALU.mult))
                assert count[0] == LN_OPS

            def ln_out(g):
                dve.tensor_scalar(y[:, g], y[:, g], mv[:, g, 0:1], rs[:, g:g + 1],
                                  ALU.subtract, ALU.mult).then_inc(ln_done, 1)

            def step(u, b, j, first=False, finish=None, with_scores=True, ahead=True):
                if finish is not None:
                    take_out(finish)
                for g in range(3):
                    if with_scores:
                        masked(b + 1, j, u + NB, g)
                    if g == 0:
                        sums(u, first)
                    if finish is not None and g < 2:
                        ln_stats(finish, 2 * g)
                        ln_stats(finish, 2 * g + 1)
                if finish is not None:
                    ln_scale(finish)
                parts(u, j, 0)
                parts(u, j, 1)
                if with_scores:
                    masked(b + 1, j, u + NB, 3)
                parts(u, j, 2)
                if ahead:
                    split_lo(0, KEY0 + NB + u + 1)
                parts(u, j, 3)
                if with_scores:
                    maximum(j, u + NB, first)
                if finish is not None:
                    for g in range(G):
                        ln_out(g)

            dve.wait_ge(lo_done, KEY0 + 1)

            def first_scores(k, t, first=False):
                split_lo(1 - k, KEY0 + t + 1)
                for g in range(G):
                    masked(0, t, t, g)
                maximum(t, t, first)

            first_scores(0, 0, True)
            first_scores(1, 1)
            with dve.Fori(1, NB // 2) as pair:
                for k in range(2):
                    first_scores(k, 2 * pair + k)
            block_maximum(0)
            step(0, 0, 0, first=True)
            with dve.Fori(0, NB - 2) as b:
                with dve.Fori(1, NB) as j:
                    step(dve.snap(NB * b + j), b, j)
                block_maximum(b + 1)
                step(dve.snap(NB * b + NB), b + 1, 0, first=True, finish=b)
            with dve.Fori(1, NB - 1) as j:
                step(dve.snap(NB * (NB - 2) + j), NB - 2, j)
            step(NB * (NB - 1) - 1, NB - 2, NB - 1, ahead=False)
            block_maximum(NB - 1)
            step(NB * (NB - 1), NB - 1, 0, first=True, finish=NB - 2, with_scores=False, ahead=False)
            with dve.Fori(1, NB) as j:
                step(dve.snap(NB * (NB - 1) + j), NB - 1, j, with_scores=False, ahead=False)
            take_out(NB - 1)
            for g in range(G):
                ln_stats(NB - 1, g)
            ln_scale(NB - 1)
            for g in range(G):
                ln_out(g)


def kernel(x, adj, L0_gnn_key, L0_gnn_value, L0_gnn_Wq, L0_gnn_bq, L0_gnn_Wk, L0_gnn_bk,
           L0_gnn_Wv, L0_gnn_bv, L0_gnn_Wm, L0_gnn_bm):
    import numpy as _np
    import concourse.bacc as _bacc
    from concourse.bass_utils import run_bass_kernel_spmd as _run

    def tiles(a):
        a = _np.asarray(a).reshape(NB, W, C, P)
        return _np.ascontiguousarray(a.transpose(0, 3, 2, 1))

    def column(a):
        return _np.ascontiguousarray(_np.asarray(a).reshape(C, P).T)

    arrays = {
        "x": _np.ascontiguousarray(x), "adj": _np.ascontiguousarray(adj),
        "xT": tiles(x), "keyT": tiles(L0_gnn_key), "valT": tiles(L0_gnn_value),
        "Wq": _np.ascontiguousarray(L0_gnn_Wq), "Wk": _np.ascontiguousarray(L0_gnn_Wk),
        "Wv": _np.ascontiguousarray(L0_gnn_Wv), "WmT": _np.ascontiguousarray(_np.asarray(L0_gnn_Wm).T),
        "bq": column(L0_gnn_bq), "bk": column(L0_gnn_bk), "bv": column(L0_gnn_bv),
        "bm": _np.ascontiguousarray(_np.asarray(L0_gnn_bm).reshape(1, D)),
        "ident": _np.eye(P, dtype=_np.float32),
    }
    nc = _bacc.Bacc("TRN2", target_bir_lowering=False, num_devices=1, dynamic_dma_scratch_size=1024)
    args = [nc.dram_tensor(f"in_{n}_dram", a.shape, F32, kind="ExternalInput").ap() for n, a in arrays.items()]
    q_scratch = nc.dram_tensor("q_scratch", (NB, P, C, 2, W), F32, kind="Internal").ap()
    out = nc.dram_tensor("out_dram", (N, D), F32, kind="ExternalOutput").ap()
    gnn_attention_kernel(nc, *args, q_scratch, out)
    r = _run(nc, [{f"in_{n}_dram": a for n, a in arrays.items()}], core_ids=[0])
    return r.results[0]["out_dram"]
```

```python
from contextlib import ExitStack

import concourse.bass as bass
from concourse import mybir

ALU = mybir.AluOpType
ACT = mybir.ActivationFunctionType
AX = mybir.AxisListType
F32 = mybir.dt.float32
F32R = mybir.dt.float32r
BF16 = mybir.dt.bfloat16
I32 = mybir.dt.int32

P = 128
N = 4096
D = 512
C = D // P
W = 512
G = W // P
NB = N // W
SCALE = 1.0 / float(N) ** 0.5
CUT = 1e-5
MASKED = -1e9
EPS = 1e-5
LN_OPS = 5 + 3 * 3


def gnn_attention_kernel(nc, x, adj, xT, keyT, valT, Wq, Wk, Wv, WmT, bq, bk, bv, bm, ident_in,
                         q_scratch, out):
    adj_t = adj.rearrange("(b g p) (j m) -> b j g p m", g=G, p=P, m=W)
    x_t = x.rearrange("(b g p) d -> b p g d", g=G, p=P)
    out_t = out.rearrange("(b g p) d -> b p g d", g=G, p=P)

    with ExitStack() as ctx:
        def sb(name, shape, dt=F32, where=ctx):
            return where.enter_context(nc.sbuf_tensor(name, [P] + shape, dt))

        def sem(name):
            return ctx.enter_context(nc.semaphore(name))

        acc = ctx.enter_context(nc.psum_tensor("acc", [P, G, W], F32))
        ps_s = ctx.enter_context(nc.psum_tensor("ps_s", [P, 2, W], F32))
        ps_t = ctx.enter_context(nc.psum_tensor("ps_t", [P, 2, W], F32))

        ident = sb("ident", [P])
        ones = sb("ones", [P])
        bq_c, bk_c, bv_c = sb("bq_c", [C]), sb("bk_c", [C]), sb("bv_c", [C])
        qbias = sb("qbias", [C])
        rbias = sb("rbias", [1])
        r_new = sb("r_new", [G])
        r_all = sb("r_all", [NB * G])
        mx, mx_tile, neg_mx = sb("mx", [G]), sb("mx_tile", [G]), sb("neg_mx", [G])
        esum, rowsum, rinv = sb("esum", [G]), sb("rowsum", [G]), sb("rinv", [G])
        ysum, ysq = sb("ysum", [G]), sb("ysq", [G])
        neg_mean, shift = sb("neg_mean", [G]), sb("shift", [G])
        ve, rs, nt = sb("ve", [G]), sb("rs", [G]), sb("nt", [G])
        raw = [sb("raw0", [C, W])]
        hi = [sb("hi0", [C, W], F32R)]
        lo = [sb("lo0", [C, W], F32R)]
        q_hl = sb("q_hl", [C, 2, W], F32R)
        adj_s = sb("adj_s", [G, W])
        mag = sb("mag", [2, W])
        cut = sb("cut", [W], BF16)
        wvm_h = sb("wvm_h", [C, D], F32R)
        with ExitStack() as early:
            vbias = sb("vbias", [D], F32, early)
        y = sb("y", [G, W])

        with ExitStack() as early:
            vbias_early = sb("vbias_early", [D], F32, early)
            w1 = sb("w1", [D], F32, early)
            m_h, m_l = (sb(n, [C, D], F32R, early) for n in ("m_h", "m_l"))
            q_out = sb("q_out", [C, 2, W], F32R, early)
            wq_s, wk_s, wv_s, wm_s = (sb(n, [C, D], F32, early) for n in ("wq_s", "wk_s", "wv_s", "wm_s"))
            bk_r, bv_r = sb("bk_r", [C, P], F32, early), sb("bv_r", [C, P], F32, early)
            bm_r = sb("bm_r", [D], F32, early)
            sb("unused", [128 * 256 - (2 * D + 8 * C * D + 2 * C * P + D) - C * D], F32, early)
            wvm_l = sb("wvm_l", [C, D], F32R, early)
        t_s = sb("t_s", [G, NB, W])
        v_s = sb("v_s", [NB * G, D])

        with ExitStack() as stream:
            raw.append(sb("raw1", [C, W], F32, stream))
            hi.append(sb("hi1", [C, W], F32R, stream))
            lo.append(sb("lo1", [C, W], F32R, stream))
        prob = sb("prob", [G, W])
        p_h, p_l = sb("p_h", [2, W], F32R), sb("p_l", [2, W], F32R)
        v_h, v_l = sb("v_h", [2, D], F32R), sb("v_l", [2, D], F32R)

        wqk_in, wvm_in = sem("wqk_in"), sem("wvm_in")
        raw_in = [sem("raw_in0"), sem("raw_in1")]
        y_in = sem("y_in")
        q_in = sem("q_in")
        adj_in = [sem(f"adj_in{g}") for g in range(G)]
        q_stored = [sem(f"q_stored{c}") for c in range(C)]
        out_stored = sem("out_stored")
        reps = sem("reps")
        wmm = sem("wmm")
        w_hi = sem("w_hi")
        hi_done, lo_done = sem("hi_done"), sem("lo_done")
        group = sem("group")
        acc_free = sem("acc_free")
        q_hi = sem("q_hi")
        bias_moved = sem("bias_moved")
        r_part, r_done = sem("r_part"), sem("r_done")
        s_read = sem("s_read")
        mag_done = sem("mag_done")
        cut_done, t_done = sem("cut_done"), sem("t_done")
        mx_part, mx_done = sem("mx_part"), sem("mx_done")
        exp_done = sem("exp_done")
        sum_done = sem("sum_done")
        turned = sem("turned")
        ph_done, pl_done = sem("ph_done"), sem("pl_done")
        vh_done, vl_done = sem("vh_done"), sem("vl_done")
        pv_done = sem("pv_done")
        rinv_done = sem("rinv_done")
        acc_read = sem("acc_read")
        ln_op = sem("ln_op")
        sq_done = sem("sq_done")
        kh_done = sem("kh_done")
        ln_done = sem("ln_done")

        KEY0 = 2 * NB
        block = ctx.enter_context(nc.Block())

        @block.sync
        def _(sp):
            for dst, src in ((wq_s, Wq), (wk_s, Wk)):
                sp.dma_start(dst[:], src.rearrange("(c p) d -> p c d", p=P)).then_inc(wqk_in, 16)
            for dst, src in ((bq_c, bq), (bk_c, bk)):
                sp.dma_start(dst[:], src).then_inc(wqk_in, 16)
            sp.dma_start(raw[0][:], xT[0]).then_inc(raw_in[0], 16)
            for dst, src in ((wv_s, Wv), (wm_s, WmT)):
                sp.dma_start(dst[:], src.rearrange("(c p) d -> p c d", p=P)).then_inc(wvm_in, 16)
            for dst, src in ((bv_c[:], bv), (bm_r[0:1, :], bm), (ident[:], ident_in)):
                sp.dma_start(dst, src).then_inc(wvm_in, 16)
            sp.dma_start(raw[1][:], xT[1]).then_inc(raw_in[1], 16)
            sp.dma_start(y[:], x_t[0]).then_inc(y_in, 16)

            def load_raw(k, tile, number):
                sp.wait_ge(lo_done, number - 1)
                sp.dma_start(raw[k][:], tile).then_inc(raw_in[k], 16)

            def store_q(b):
                for c in range(C):
                    sp.wait_ge(acc_free, 2 * C + 4 * b + c + 1)
                    sp.dma_start(q_scratch[b, :, c], q_out[:, c].bitcast(F32)).then_inc(q_stored[c], 16)

            def x_rows(b):
                sp.wait_ge(r_done, b + 1)
                sp.dma_start(y[:], x_t[b + 1]).then_inc(y_in, 16)

            with sp.Fori(0, NB // 2 - 1) as pair:
                for k in range(2):
                    load_raw(k, xT[2 * pair + k + 2], 2 * pair + k + 2)
                    x_rows(2 * pair + k)
                    store_q(2 * pair + k)
            load_raw(0, valT[0], NB)
            x_rows(NB - 2)
            store_q(NB - 2)
            load_raw(1, keyT[0], NB + 1)
            store_q(NB - 1)
            for c in range(C):
                sp.wait_ge(q_stored[c], 16 * NB)
            sp.dma_start(q_hl[:].bitcast(F32), q_scratch[0]).then_inc(q_in, 16)
            for g in range(G):
                sp.dma_start(adj_s[:, g], adj_t[0, 0, g]).then_inc(adj_in[g], 16)

            def load_adj(b, j, t, groups=range(G)):
                for g in groups:
                    sp.wait_ge(t_done, 4 * t + g - 3)
                    sp.dma_start(adj_s[:, g], adj_t[b, j, g]).then_inc(adj_in[g], 16)

            def load_key(j, t):
                sp.wait_ge(lo_done, KEY0 + t)
                sp.dma_start(raw[0][:], keyT[j]).then_inc(raw_in[0], 16)

            with sp.Fori(1, NB) as j:
                load_raw(0, valT[j], 2 * j + NB)
                load_raw(1, keyT[j], 2 * j + NB + 1)
                load_adj(0, j, j)
            load_raw(0, keyT[0], KEY0 + NB)
            sp.wait_ge(acc_free, 2 * C + 8 * NB)
            sp.dma_start(y[:], x_t[0]).then_inc(y_in, 16)

            def open_block(b):
                load_adj(b, 0, NB * b, range(3))
                sp.wait_ge(group, 4 * KEY0 + 4 * NB * b)
                sp.dma_start(q_hl[:].bitcast(F32), q_scratch[b]).then_inc(q_in, 16)
                load_adj(b, 0, NB * b, range(3, G))
                load_key(1, NB * b + 1)
                load_adj(b, 1, NB * b + 1)

            def turn_y(b):
                sp.wait_ge(ln_done, 4 * b + 4)
                sp.dma_start(out_t[b], y[:]).then_inc(out_stored, 16)
                sp.wait_ge(out_stored, 16 * b + 16)

            def rest(b):
                with sp.Fori(2, NB) as j:
                    t = sp.snap(NB * b + j)
                    load_key(j, t)
                    load_adj(b, j, t)

            open_block(1)
            rest(1)
            with sp.Fori(2, NB) as b:
                load_key(0, NB * b)
                open_block(b)
                turn_y(b - 2)
                sp.dma_start(y[:], x_t[b - 1]).then_inc(y_in, 16)
                rest(b)
            turn_y(NB - 2)
            sp.dma_start(y[:], x_t[NB - 1]).then_inc(y_in, 16)
            turn_y(NB - 1)

        @block.tensor
        def _(pe):
            def times(out, a, b, start, stop, last=True):
                n = len(a)
                for i, ((ah, al), (bh, bl)) in enumerate(zip(a, b)):
                    pe.matmul(out, ah, bh, start=start and i == 0, stop=False, skip_group_check=True)
                    pe.matmul(out, ah, bl, start=False, stop=False, skip_group_check=True)
                    mm = pe.matmul(out, al, bh, start=False, stop=stop and i == n - 1, skip_group_check=True)
                return mm

            pe.wait_ge(wqk_in, 64)
            for c in range(C):
                for o in range(C):
                    mm = pe.matmul(acc[:, c], wq_s[:, o, c * P:(c + 1) * P], wk_s[:, o], start=o == 0, stop=o == C - 1)
                mm.then_inc(wmm, 1)
            pe.wait_ge(wvm_in, 80)
            for c in range(C):
                bank = (ps_s if c < 2 else ps_t)[:, c % 2]
                for o in range(C):
                    mm = pe.matmul(bank, wv_s[:, o, c * P:(c + 1) * P], wm_s[:, o], start=o == 0, stop=o == C - 1)
                mm.then_inc(wmm, 1)
            pe.wait_ge(reps, 2)
            pe.wait_ge(acc_free, 1)
            for o in range(C):
                mm = pe.matmul(acc[:, 0], bk_r[:, o], wq_s[:, o], start=o == 0, stop=o == C - 1)
            mm.then_inc(wmm, 1)
            pe.wait_ge(acc_free, 2)
            for o in range(C):
                pe.matmul(acc[:, 1], bv_r[:, o], wm_s[:, o], start=o == 0, stop=False)
            pe.matmul(acc[:, 1], ones[0:1, :], bm_r[0:1, :], start=False, stop=True).then_inc(wmm, 1)
            pe.wait_ge(acc_free, 3)
            for c in range(C):
                for o in range(C):
                    mm = pe.matmul(acc[:, 2, c:c + 1], wk_s[:, o, c * P:(c + 1) * P], bq_c[:, o:o + 1],
                                   start=o == 0, stop=o == C - 1)
            mm.then_inc(wmm, 1)
            pe.wait_ge(acc_free, 4)
            for o in range(C):
                mm = pe.matmul(acc[:, 3, 0:1], bk_r[:, o], bq_c[:, o:o + 1], start=o == 0, stop=o == C - 1)
            mm.then_inc(wmm, 1)

            def project_x(k, b):
                pe.wait_ge(lo_done, b + 1)
                for e in range(C):
                    pe.wait_ge(acc_free, 4 * b + e + 5)
                    cols = slice(e * P, (e + 1) * P)
                    times(acc[:, e], [(m_h[:, c, cols], m_l[:, c, cols]) for c in range(C)],
                          [(hi[k][:, c], lo[k][:, c]) for c in range(C)], True, True).then_inc(group, 1)

            with pe.Fori(0, NB // 2) as pair:
                for k in range(2):
                    project_x(k, 2 * pair + k)

            def project_value(k, j):
                pe.wait_ge(lo_done, NB + 2 * j + 1)
                for e in range(G):
                    pe.wait_ge(acc_free, 4 * NB + 4 * j + e + 5)
                    cols = slice(e * P, (e + 1) * P)
                    times(acc[:, e], [(hi[k][:, c, cols], lo[k][:, c, cols]) for c in range(C)],
                          [(wvm_h[:, c], wvm_l[:, c]) for c in range(C)], True, True).then_inc(group, 1)

            def scores(k, t, g, number):
                if g == 0:
                    pe.wait_ge(lo_done, number + 1)
                pe.wait_ge(s_read, 4 * t + g + 1)
                rows = slice(g * P, (g + 1) * P)
                times(ps_s[:, g % 2], [(q_hl[:, c, 0, rows], q_hl[:, c, 1, rows]) for c in range(C)],
                      [(hi[k][:, c], lo[k][:, c]) for c in range(C)], True, True).then_inc(group, 1)

            def turn(u, c):
                if c == 0:
                    pe.wait_ge(exp_done, 4 * u + 4)
                for g in range(G):
                    mm = pe.transpose(ps_t[:, c % 2, g * P:(g + 1) * P], prob[:, g, c * P:(c + 1) * P], ident[:])
                mm.then_inc(turned, 1)

            def product(u, c, first):
                pe.wait_ge(pl_done, 4 * u + c + 1)
                pe.wait_ge(vl_done, 4 * u + c + 1)
                for g in range(G):
                    rows = slice(g * P, (g + 1) * P)
                    mm = times(acc[:, g], [(p_h[:, c % 2, rows], p_l[:, c % 2, rows])],
                               [(v_h[:, c % 2], v_l[:, c % 2])], first and c == 0, False)
                mm.then_inc(pv_done, 1)

            def step(u, first=False, results=None):
                for g in range(3):
                    scores(0, u + NB, g, KEY0 + NB + u)
                turn(u, 0)
                scores(0, u + NB, 3, KEY0 + NB + u)
                turn(u, 1)
                if results is not None:
                    pe.wait_ge(sq_done, results)
                for c in range(4):
                    product(u, c, first)
                    if c < 2:
                        turn(u, c + 2)

            def last_step(u, first=False, more=True):
                if first:
                    pe.wait_ge(sq_done, 4 * (NB - 1))
                for c in range(4):
                    product(u, c, first)
                    if c < 2:
                        turn(u, c + 2)
                    elif more:
                        turn(u + 1, c - 2)

            with pe.Fori(0, NB) as j:
                project_value(0, j)
                for g in range(G):
                    if g == 0:
                        pe.wait_ge(q_in, 16)
                    scores(1, j, g, NB + 1 + 2 * j)
            pe.wait_ge(q_in, 32)
            step(0, first=True)
            with pe.Fori(0, NB - 2) as b:
                with pe.Fori(1, NB) as j:
                    step(pe.snap(NB * b + j))
                pe.wait_ge(q_in, 16 * b + 48)
                step(pe.snap(NB * b + NB), first=True, results=4 * b + 4)
            with pe.Fori(1, NB) as j:
                step(pe.snap(NB * (NB - 2) + j))
            last = NB * (NB - 1)
            turn(last, 0)
            turn(last, 1)
            last_step(last, first=True)
            with pe.Fori(1, NB - 1) as j:
                last_step(pe.snap(last + j))
            last_step(last + NB - 1, more=False)

        @block.scalar
        def _(act):
            def split_hi(k, number, loads, groups, pieces=range(1)):
                act.wait_ge(raw_in[k], 16 * loads)
                if groups is not None:
                    act.wait_ge(group, groups)
                act.activation(hi[k][:], raw[k][:], ACT.Copy).then_inc(hi_done, 1)

            split_hi(0, 0, 1, None)
            for c in range(C):
                act.wait_ge(wmm, c + 1)
                act.activation(m_h[:, c], acc[:, c], ACT.Copy, scale=SCALE).then_inc(w_hi, 1)
            for c in range(C):
                act.wait_ge(wmm, C + c + 1)
                act.activation(wvm_h[:, c], (ps_s if c < 2 else ps_t)[:, c % 2], ACT.Copy).then_inc(w_hi, 1)

            def q_parts(b):
                for c in range(C):
                    act.wait_ge(group, 4 * b + c + 1)
                    if not (isinstance(b, int) and b == 0):
                        act.wait_ge(q_stored[c], 16 * b)
                    act.activation(q_out[:, c, 0], acc[:, c], ACT.Identity, bias=qbias[:, c:c + 1]).then_inc(q_hi, 1)

            act.wait_ge(acc_free, 2 * C)
            split_hi(1, 1, 1, None)
            q_parts(0)
            split_hi(0, 2, 2, 4)
            q_parts(1)
            with act.Fori(1, NB // 2) as pair:
                for k in range(2):
                    b = 2 * pair + k
                    split_hi(1 - k, b + 1, pair + 1 + k, 4 * b)
                    q_parts(b)
            def magnitude(t, g):
                act.wait_ge(s_read, 4 * t + g + 3)
                act.activation(mag[:, g % 2], adj_s[:, g], ACT.Abs).then_inc(mag_done, 1)

            def exps(u, b, j):
                act.wait_ge(mx_done, b + 1)
                act.wait_ge(turned, 4 * u)
                act.wait_ge(sum_done, u)
                for g in range(G):
                    act.activation(prob[:, g], t_s[:, g, j], ACT.Exp, bias=neg_mx[:, g:g + 1],
                                   accum_out=esum[:, g:g + 1]).then_inc(exp_done, 1)

            def v_part(u, j, c):
                if not (isinstance(u, int) and u == 0 and c < 2):
                    act.wait_ge(pv_done, 4 * u + c - 1)
                act.activation(v_h[:, c % 2], v_s[:, 4 * j + c], ACT.Copy).then_inc(vh_done, 1)

            def p_part(u, c):
                act.wait_ge(turned, 4 * u + c + 1)
                act.activation(p_h[:, c % 2], ps_t[:, c % 2], ACT.Copy).then_inc(ph_done, 1)

            def key_part(u, c):
                if c == 0:
                    act.wait_ge(raw_in[0], 16 * (6 + NB + u))
                    act.wait_ge(group, 4 * KEY0 + 4 * NB + 4 + 4 * u)
                act.activation(hi[0][:, c], raw[0][:, c], ACT.Copy).then_inc(kh_done, 1)

            def squares(b, g):
                if g == 0:
                    act.wait_ge(ln_op, LN_OPS * b + 1)
                act.activation(acc[:, g], y[:, g], ACT.Square, bias=neg_mean[:, g:g + 1],
                               accum_out=ysq[:, g:g + 1]).then_inc(sq_done, 1)

            def normalised(b):
                act.wait_ge(ln_op, LN_OPS * b + LN_OPS)
                for g in range(G):
                    act.activation(y[:, g], y[:, g], ACT.Identity, bias=shift[:, g:g + 1],
                                   scale=rs[:, g:g + 1]).then_inc(ln_done, 1)

            def step(u, b, j, finish=None, with_scores=True, ahead=True):
                if with_scores:
                    v_part(u, j, 0)
                    v_part(u, j, 1)
                exps(u, b, j)
                if finish is not None:
                    squares(finish, 0)
                    squares(finish, 1)
                if with_scores:
                    magnitude(u + NB, 0)
                if finish is not None:
                    squares(finish, 2)
                    squares(finish, 3)
                if with_scores:
                    magnitude(u + NB, 1)
                    p_part(u, 0)
                    magnitude(u + NB, 2)
                    p_part(u, 1)
                    magnitude(u + NB, 3)
                else:
                    for c in range(2):
                        v_part(u, j, c)
                        p_part(u, c)
                if ahead:
                    key_part(u, 0)
                    key_part(u, 1)
                v_part(u, j, 2)
                p_part(u, 2)
                if ahead:
                    key_part(u, 2)
                    key_part(u, 3)
                v_part(u, j, 3)
                p_part(u, 3)
                if finish is not None:
                    normalised(finish)

            with act.Fori(0, NB) as j:
                split_hi(1, None, j + NB // 2 + 1, 8 * j + 4 * NB)
                split_hi(0, None, j + NB // 2 + 2, 8 * j + 4 * NB + 4)
                for g in range(G):
                    magnitude(j, g)
            step(0, 0, 0)
            with act.Fori(0, NB - 2) as b:
                with act.Fori(1, NB) as j:
                    step(act.snap(NB * b + j), b, j)
                step(act.snap(NB * b + NB), b + 1, 0, finish=b)
            with act.Fori(1, NB - 1) as j:
                step(act.snap(NB * (NB - 2) + j), NB - 2, j)
            step(NB * (NB - 1) - 1, NB - 2, NB - 1, ahead=False)
            step(NB * (NB - 1), NB - 1, 0, finish=NB - 2, with_scores=False, ahead=False)
            with act.Fori(1, NB) as j:
                step(act.snap(NB * (NB - 1) + j), NB - 1, j, with_scores=False, ahead=False)
            for g in range(G):
                squares(NB - 1, g)
            normalised(NB - 1)

        @block.vector
        def _(dve):
            def minus_hi(lo_part, whole, hi_part):
                return dve.tensor_tensor(lo_part, whole, hi_part.bitcast(F32), ALU.subtract)

            def split_lo(k, number):
                dve.wait_ge(hi_done, number + 1)
                minus_hi(lo[k][:], raw[k][:], hi[k][:]).then_inc(lo_done, 1)

            dve.memset(ones[:], 1.0).then_inc(reps, 1)
            dve.wait_ge(wqk_in, 64)
            dve.wait_ge(wvm_in, 80)
            dve.wait_ge(reps, 1)
            for o in range(C):
                dve.tensor_scalar(bk_r[:, o], ones[:], bk_c[:, o:o + 1], None, ALU.mult)
                last = dve.tensor_scalar(bv_r[:, o], ones[:], bv_c[:, o:o + 1], None, ALU.mult)
            last.then_inc(reps, 1)
            split_lo(0, 0)
            for c in range(C):
                dve.wait_ge(w_hi, c + 1)
                dve.scalar_tensor_tensor(m_l[:, c], acc[:, c], SCALE, m_h[:, c].bitcast(F32),
                                         ALU.mult, ALU.subtract).then_inc(acc_free, 1)
            for c in range(C):
                dve.wait_ge(w_hi, C + c + 1)
                low = minus_hi(wvm_l[:, c], (ps_s if c < 2 else ps_t)[:, c % 2], wvm_h[:, c])
                if c < 2:
                    low.then_inc(s_read, 1)
            dve.wait_ge(wmm, 2 * C + 1)
            dve.tensor_scalar(w1[:], acc[:, 0], SCALE, None, ALU.mult).then_inc(acc_free, 1)
            dve.wait_ge(wmm, 2 * C + 2)
            dve.tensor_copy(vbias_early[:], acc[:, 1]).then_inc(acc_free, 1)
            dve.wait_ge(wmm, 2 * C + 3)
            dve.tensor_scalar(qbias[:], acc[:, 2, 0:C], SCALE, None, ALU.mult).then_inc(acc_free, 1)
            dve.wait_ge(wmm, 2 * C + 4)
            dve.tensor_scalar(rbias[:], acc[:, 3, 0:1], SCALE, None, ALU.mult).then_inc(acc_free, 1)
            dve.wait_ge(acc_free, 2 * C)

            with dve.Fori(0, NB // 2) as pair:
                for k in range(2):
                    b = 2 * pair + k
                    split_lo(1 - k, b + 1)
                    dve.wait_ge(y_in, 16 * b + 16)
                    for g in range(G):
                        dve.tensor_tensor_reduce(y[:, g], y[:, g], w1[:], 1.0, 0.0, ALU.mult, ALU.add,
                                                 r_new[:, g:g + 1]).then_inc(r_part, 1)
                    dve.wait_ge(r_part, 4 * b + 4)
                    dve.tensor_scalar(r_all[:, bass.ds(4 * b, G)], r_new[:], rbias[:, 0:1], None,
                                      ALU.add).then_inc(r_done, 1)
                    for c in range(C):
                        dve.wait_ge(q_hi, 4 * b + c + 1)
                        dve.scalar_tensor_tensor(q_out[:, c, 1], acc[:, c], qbias[:, c:c + 1],
                                                 q_out[:, c, 0].bitcast(F32), ALU.add,
                                                 ALU.subtract).then_inc(acc_free, 1)

            dve.wait_ge(r_done, NB)
            dve.tensor_copy(vbias[:], vbias_early[:]).then_inc(bias_moved, 1)
            dve.wait_ge(bias_moved, 1)

            def v_tile(j, last=False):
                for c in range(G):
                    dve.wait_ge(group, 4 * NB + 8 * j + (G if last else c + 1))
                    dve.tensor_tensor(v_s[:, bass.ds(4 * j + c, 1)], acc[:, c], vbias[:], ALU.add).then_inc(acc_free, 1)

            def weighted(b, t, g, groups):
                dve.wait_ge(group, groups)
                dve.wait_ge(adj_in[g], 16 * t + 16)
                dve.scalar_tensor_tensor(adj_s[:, g], ps_s[:, g % 2], r_all[:, bass.ds(4 * b + g, 1)],
                                         adj_s[:, g], ALU.add, ALU.mult).then_inc(s_read, 1)

            def masked(j, t, g):
                dve.wait_ge(mag_done, 4 * t + g + 1)
                dve.tensor_scalar(cut[:], mag[:, g % 2], CUT, None, ALU.is_lt).then_inc(cut_done, 1)
                dve.wait_ge(cut_done, 4 * t + g + 1)
                dve.scalar_tensor_tensor(t_s[:, g, j], cut[:], MASKED, adj_s[:, g],
                                         ALU.mult, ALU.add).then_inc(t_done, 1)

            def tile_maximum(j, g, first):
                dve.drain()
                dve.tensor_reduce((mx if first else mx_tile)[:, g:g + 1], t_s[:, g, j], AX.X,
                                  ALU.max).then_inc(mx_part, 2 if first and g == G - 1 else 1)

            def maximum(t, first=False):
                if not first:
                    dve.wait_ge(mx_part, 5 * t + 4)
                    dve.tensor_tensor(mx[:], mx[:], mx_tile[:], ALU.max).then_inc(mx_part, 1)

            def block_maximum(b):
                dve.wait_ge(mx_part, 5 * NB * (b + 1))
                dve.tensor_scalar(neg_mx[:], mx[:], -1.0, None, ALU.mult).then_inc(mx_done, 1)

            def v_part(u, j, c):
                dve.wait_ge(vh_done, 4 * u + c + 1)
                minus_hi(v_l[:, c % 2], v_s[:, 4 * j + c], v_h[:, c % 2]).then_inc(vl_done, 1)

            def p_part(u, c):
                dve.wait_ge(ph_done, 4 * u + c + 1)
                minus_hi(p_l[:, c % 2], ps_t[:, c % 2], p_h[:, c % 2]).then_inc(pl_done, 1)

            def key_part(u, c):
                dve.wait_ge(kh_done, 4 * u + c + 1)
                low = minus_hi(lo[0][:, c], raw[0][:, c], hi[0][:, c])
                if c == C - 1:
                    low.then_inc(lo_done, 1)

            def sums(u, first):
                dve.wait_ge(exp_done, 4 * u + 4)
                if first:
                    dve.tensor_copy(rowsum[:], esum[:]).then_inc(sum_done, 1)
                else:
                    dve.wait_ge(sum_done, u)
                    dve.tensor_tensor(rowsum[:], rowsum[:], esum[:], ALU.add).then_inc(sum_done, 1)

            def take_out(b, g):
                if g == 0:
                    dve.wait_ge(sum_done, NB * b + NB)
                    dve.reciprocal(rinv[:], rowsum[:]).then_inc(rinv_done, 1)
                    dve.wait_ge(rinv_done, b + 1)
                    dve.wait_ge(pv_done, 4 * NB * b + 4 * NB)
                    dve.wait_ge(y_in, 16 * (NB + b + 1))
                dve.scalar_tensor_tensor(y[:, g], acc[:, g], rinv[:, g:g + 1], y[:, g], ALU.mult, ALU.add,
                                         accum_out=ysum[:, g:g + 1]).then_inc(acc_read, 1)

            def ln_step(b, n):
                if n == 1:
                    dve.wait_ge(acc_read, 4 * b + 4)
                    step_n = dve.tensor_scalar(neg_mean[:], ysum[:], -1.0 / D, None, ALU.mult)
                elif n == 2:
                    dve.wait_ge(sq_done, 4 * b + 4)
                    step_n = dve.tensor_scalar(ve[:], ysq[:], 1.0 / D, EPS, ALU.mult, ALU.add)
                else:
                    dve.wait_ge(ln_op, LN_OPS * b + n - 1)
                    if n == 3:
                        step_n = dve.tensor_scalar(nt[:].bitcast(I32), ve[:].bitcast(I32), 1, None,
                                                   ALU.arith_shift_right)
                    elif n == 4:
                        step_n = dve.tensor_scalar(rs[:].bitcast(I32), nt[:].bitcast(I32), -1.0,
                                                   float(0x5f3759df), ALU.mult, ALU.add)
                    elif n == LN_OPS:
                        step_n = dve.tensor_tensor(shift[:], neg_mean[:], rs[:], ALU.mult)
                    elif n % 3 == 2:
                        step_n = dve.scalar_tensor_tensor(nt[:], rs[:], -0.5, rs[:], ALU.mult, ALU.mult)
                    elif n % 3 == 0:
                        step_n = dve.tensor_tensor(nt[:], nt[:], ve[:], ALU.mult)
                    else:
                        step_n = dve.scalar_tensor_tensor(rs[:], nt[:], 1.5, rs[:], ALU.add, ALU.mult)
                step_n.then_inc(ln_op, 1)

            def ln_steps(b, steps):
                if b is not None:
                    for n in steps:
                        ln_step(b, n)

            def step(u, b, j, first=False, finish=None, ahead=True):
                t = u + NB
                scored = 4 * KEY0 + 4 * NB + 4 * u
                if finish is not None:
                    take_out(finish, 0)
                    take_out(finish, 1)
                v_part(u, j, 0)
                if finish is None:
                    v_part(u, j, 1)
                weighted(b + 1, t, 0, scored + 1)
                if finish is not None:
                    take_out(finish, 2)
                    take_out(finish, 3)
                    ln_step(finish, 1)
                sums(u, first)
                masked(j, t, 0)
                weighted(b + 1, t, 1, scored + 2)
                if finish is not None:
                    v_part(u, j, 1)
                tile_maximum(j, 0, first)
                masked(j, t, 1)
                weighted(b + 1, t, 2, scored + 3)
                tile_maximum(j, 1, first)
                p_part(u, 0)
                masked(j, t, 2)
                weighted(b + 1, t, 3, scored + 4)
                ln_steps(finish, (2,))
                p_part(u, 1)
                ln_steps(finish, (3,))
                tile_maximum(j, 2, first)
                ln_steps(finish, (4,))
                masked(j, t, 3)
                ln_steps(finish, (5,))
                tile_maximum(j, 3, first)
                ln_steps(finish, (6,))
                v_part(u, j, 2)
                ln_steps(finish, (7,))
                p_part(u, 2)
                ln_steps(finish, (8,))
                if ahead:
                    for c in range(2):
                        key_part(u, c)
                        ln_steps(finish, (9 + c,))
                v_part(u, j, 3)
                ln_steps(finish, (11,))
                p_part(u, 3)
                ln_steps(finish, (12,))
                if ahead:
                    for c in range(2, 4):
                        key_part(u, c)
                        ln_steps(finish, (11 + c,))
                maximum(t, first)

            def last_step(u, j, first=False, finish=None):
                if finish is not None:
                    for g in range(G):
                        take_out(finish, g)
                    ln_step(finish, 1)
                sums(u, first)
                for c in range(4):
                    v_part(u, j, c)
                    p_part(u, c)
                ln_steps(finish, range(2, LN_OPS + 1))

            def first_scores(j, first=False, last=False):
                split_lo(1, NB + 2 * j + 1)
                v_tile(j, last)
                split_lo(0, NB + 2 * j + 2)
                for g in range(G):
                    weighted(0, j, g, 4 * NB + 4 + 8 * j + g + 1)
                    if g:
                        tile_maximum(j, g - 1, first)
                    masked(j, j, g)
                tile_maximum(j, G - 1, first)
                maximum(j, first)

            first_scores(0, first=True)
            with dve.Fori(1, NB - 1) as j:
                first_scores(j)
            first_scores(NB - 1, last=True)
            block_maximum(0)
            step(0, 0, 0, first=True)
            with dve.Fori(0, NB - 2) as b:
                with dve.Fori(1, NB) as j:
                    step(dve.snap(NB * b + j), b, j)
                block_maximum(b + 1)
                step(dve.snap(NB * b + NB), b + 1, 0, first=True, finish=b)
            with dve.Fori(1, NB - 1) as j:
                step(dve.snap(NB * (NB - 2) + j), NB - 2, j)
            step(NB * (NB - 1) - 1, NB - 2, NB - 1, ahead=False)
            block_maximum(NB - 1)
            last_step(NB * (NB - 1), 0, first=True, finish=NB - 2)
            with dve.Fori(1, NB) as j:
                last_step(dve.snap(NB * (NB - 1) + j), j)
            for g in range(G):
                take_out(NB - 1, g)
            ln_steps(NB - 1, range(1, LN_OPS + 1))


def kernel(x, adj, L0_gnn_key, L0_gnn_value, L0_gnn_Wq, L0_gnn_bq, L0_gnn_Wk, L0_gnn_bk,
           L0_gnn_Wv, L0_gnn_bv, L0_gnn_Wm, L0_gnn_bm):
    import numpy as _np
    import concourse.bacc as _bacc
    from concourse.bass_utils import run_bass_kernel_spmd as _run

    def tiles(a):
        a = _np.asarray(a).reshape(NB, W, C, P)
        return _np.ascontiguousarray(a.transpose(0, 3, 2, 1))

    def column(a):
        return _np.ascontiguousarray(_np.asarray(a).reshape(C, P).T)

    arrays = {
        "x": _np.ascontiguousarray(x), "adj": _np.ascontiguousarray(adj),
        "xT": tiles(x), "keyT": tiles(L0_gnn_key), "valT": tiles(L0_gnn_value),
        "Wq": _np.ascontiguousarray(L0_gnn_Wq), "Wk": _np.ascontiguousarray(L0_gnn_Wk),
        "Wv": _np.ascontiguousarray(L0_gnn_Wv), "WmT": _np.ascontiguousarray(_np.asarray(L0_gnn_Wm).T),
        "bq": column(L0_gnn_bq), "bk": column(L0_gnn_bk), "bv": column(L0_gnn_bv),
        "bm": _np.ascontiguousarray(_np.asarray(L0_gnn_bm).reshape(1, D)),
        "ident": _np.eye(P, dtype=_np.float32),
    }
    nc = _bacc.Bacc("TRN2", target_bir_lowering=False, num_devices=1, dynamic_dma_scratch_size=1024)
    args = [nc.dram_tensor(f"in_{n}_dram", a.shape, F32, kind="ExternalInput").ap() for n, a in arrays.items()]
    q_scratch = nc.dram_tensor("q_scratch", (NB, P, C, 2, W), F32, kind="Internal").ap()
    out = nc.dram_tensor("out_dram", (N, D), F32, kind="ExternalOutput").ap()
    gnn_attention_kernel(nc, *args, q_scratch, out)
    r = _run(nc, [{f"in_{n}_dram": a for n, a in arrays.items()}], core_ids=[0])
    return r.results[0]["out_dram"]
```

```python
from contextlib import ExitStack

import concourse.bass as bass
from concourse import mybir

ALU = mybir.AluOpType
ACT = mybir.ActivationFunctionType
AX = mybir.AxisListType
F32 = mybir.dt.float32
F32R = mybir.dt.float32r
BF16 = mybir.dt.bfloat16
I32 = mybir.dt.int32

P = 128
N = 4096
D = 512
C = D // P
W = 512
G = W // P
NB = N // W
SCALE = 1.0 / float(N) ** 0.5
CUT = 1e-5
MASKED = -1e9
EPS = 1e-5
LN_OPS = 5 + 3 * 3


def gnn_attention_kernel(nc, x, adjT, xT, key, keyT, valT, Wq, Wk, Wv, WmT, bq, bk, bv, bm, ident_in,
                         k_scratch, out):
    adj_t = adjT.rearrange("(j g p) (b m) -> b j g p m", g=G, p=P, m=W)
    x_t = x.rearrange("(b g p) d -> b p g d", g=G, p=P)
    key_t = key.rearrange("(j g p) d -> j p g d", g=G, p=P)
    out_t = out.rearrange("(b g p) d -> b p g d", g=G, p=P)

    with ExitStack() as ctx:
        def sb(name, shape, dt=F32, where=ctx):
            return where.enter_context(nc.sbuf_tensor(name, [P] + shape, dt))

        def sem(name):
            return ctx.enter_context(nc.semaphore(name))

        acc = ctx.enter_context(nc.psum_tensor("acc", [P, G, W], F32))
        ps = ctx.enter_context(nc.psum_tensor("ps", [P, G, W], F32))

        ident = sb("ident", [P])
        ones = sb("ones", [P])
        bq_c, bk_c, bv_c = sb("bq_c", [C]), sb("bk_c", [C]), sb("bv_c", [C])
        kbias = sb("kbias", [C])
        rbias = sb("rbias", [1])
        c_new = sb("c_new", [G])
        c_all = sb("c_all", [NB * G])
        vbias = sb("vbias", [D])
        mx = sb("mx", [W])
        mx_row = sb("mx_row", [G])
        mx_all = sb("mx_all", [W])
        p_sums = sb("p_sums", [W])
        rinv = sb("rinv", [G])
        ysum, ysq = sb("ysum", [G]), sb("ysq", [G])
        neg_mean, shift = sb("neg_mean", [G]), sb("shift", [G])
        ve, rs, nt = sb("ve", [G]), sb("rs", [G]), sb("nt", [G])
        k_hl = sb("k_hl", [G, C, 2, P], F32R)
        with ExitStack() as whole:
            x_in_s = sb("x_in_s", [C, 2, W], F32, whole)
        x_hl = sb("x_hl", [C, 2, W], F32R)
        adj_s = sb("adj_s", [G, W])
        mag = sb("mag", [2, W])
        cut = sb("cut", [W], BF16)
        y = sb("y", [G, W])

        with ExitStack() as early:
            m_h, m_l = (sb(n, [C, D], F32R, early) for n in ("m_h", "m_l"))
            wq_s, wk_s, wv_s, wm_s = (sb(n, [C, D], F32, early) for n in ("wq_s", "wk_s", "wv_s", "wm_s"))
            bq_r, bv_r = sb("bq_r", [C, P], F32, early), sb("bv_r", [C, P], F32, early)
            bm_r = sb("bm_r", [D], F32, early)
            hi1 = sb("hi1", [C, W], F32R, early)
            w1 = sb("w1", [D], F32, early)
            lo1 = sb("lo1", [C, W], F32R, early)
            with ExitStack() as parts:
                wq_h, wq_l, wk_h, wk_l, wm_h, wm_l = (sb(n, [C, D], F32R, parts) for n in
                                                      ("wq_h", "wq_l", "wk_h", "wk_l", "wm_h", "wm_l"))
            k_out = [sb(f"k_out{k}", [G, C, 2, P], F32R, early) for k in range(2)]
            sb("left_free", [6 * C * D - 2 * G * C * 2 * P], F32, early)
            wvm_l = sb("wvm_l", [C, D], F32R, early)
        t_s = sb("t_s", [G, NB, W])
        v_s = sb("v_s", [NB * G, D])

        with ExitStack() as stream:
            raw0 = sb("raw0", [C, W], F32, stream)
            hi0, lo0 = sb("hi0", [C, W], F32R, stream), sb("lo0", [C, W], F32R, stream)
            wvm_h = sb("wvm_h", [C, D], F32R, stream)
        prob = sb("prob", [G, W])
        p_h, p_l = sb("p_h", [G, W], F32R), sb("p_l", [G, W], F32R)
        v_h, v_l = sb("v_h", [2, D], F32R), sb("v_l", [2, D], F32R)
        raw, hi, lo = (raw0, adj_s), (hi0, hi1), (lo0, lo1)
        wv_h, wv_l = x_hl[:, :, 0], x_hl[:, :, 1]
        diag = mag[:, 0]

        wqk_in = [sem(f"wqk_in{o}") for o in range(C)]
        wvm_in = [sem(f"wvm_in{o}") for o in range(C)]
        b_in = sem("b_in")
        w_part = sem("w_part")
        w_split = sem("w_split")
        raw_in = [sem("raw_in0"), sem("raw_in1")]
        y_in = sem("y_in")
        x_in = [sem(f"x_in{c}") for c in range(C)]
        key_in = [sem(f"key_in{g}") for g in range(G)]
        adj_in = [sem(f"adj_in{g}") for g in range(G)]
        k_stored = [sem("k_stored0"), sem("k_stored1")]
        out_stored = sem("out_stored")
        reps = sem("reps")
        wmm, bias_mm = sem("wmm"), sem("bias_mm")
        w_hi = sem("w_hi")
        hi_done, lo_done = sem("hi_done"), sem("lo_done")
        group = sem("group")
        acc_free = sem("acc_free")
        k_hi = sem("k_hi")
        x_hi, x_lo = sem("x_hi"), sem("x_lo")
        c_part, c_done = sem("c_part"), sem("c_done")
        s_read = sem("s_read")
        mag_done = sem("mag_done")
        cut_done, t_done = sem("cut_done"), sem("t_done")
        mx_done = sem("mx_done")
        mx_turned = sem("mx_turned")
        mx_row_done, diag_done = sem("mx_row_done"), sem("diag_done")
        mx_spread = sem("mx_spread")
        mx_all_done = sem("mx_all_done")
        sh_done = sem("sh_done")
        exp_done = sem("exp_done")
        sum_done = sem("sum_done")
        rowsum_in = sem("rowsum_in")
        rinv_done = sem("rinv_done")
        ph_done, pl_done = sem("ph_done"), sem("pl_done")
        vh_done, vl_done = sem("vh_done"), sem("vl_done")
        pv_done = sem("pv_done")
        result = sem("result")
        acc_read = sem("acc_read")
        ln_op = sem("ln_op")
        sq_done = sem("sq_done")
        ln_done = sem("ln_done")
        norm_done = sem("norm_done")

        def valued(j, g):
            return 4 * NB + 8 * j + g + 1

        def scored(t, g, block0=False):
            if block0:
                return 4 * NB + 8 * t + g + 1 + (0 if isinstance(t, int) and t == NB - 1 else 4)
            return 12 * NB + 4 * (t - NB) + g + 1

        MX_STEPS = G * NB - 1
        block = ctx.enter_context(nc.Block())

        @block.sync
        def _(sp):
            for o in range(C):
                for dst, src in ((wq_s, Wq), (wk_s, Wk)):
                    sp.dma_start(dst[:, o], src[o * P:(o + 1) * P]).then_inc(wqk_in[o], 16)
            for dst, src in ((bq_c[:], bq), (bk_c[:], bk), (bv_c[:], bv), (bm_r[0:1, :], bm), (ident[:], ident_in)):
                sp.dma_start(dst, src).then_inc(b_in, 16)
            for o in range(C):
                for dst, src in ((wv_s, Wv), (wm_s, WmT)):
                    sp.dma_start(dst[:, o], src[o * P:(o + 1) * P]).then_inc(wvm_in[o], 16)
            for k in range(2):
                sp.dma_start(raw[k][:], keyT[k]).then_inc(raw_in[k], 16)
            sp.dma_start(y[:], key_t[0]).then_inc(y_in, 16)

            def load_raw(k, tile, freed):
                sp.wait_ge(lo_done, freed)
                sp.dma_start(raw[k][:], tile).then_inc(raw_in[k], 16)

            def store_k(k, n):
                sp.wait_ge(acc_free, 2 * C + 4 * n + 4)
                sp.dma_start(k_scratch[n], k_out[k][:].bitcast(F32)).then_inc(k_stored[k], 16)

            def load_key(j, g):
                sp.dma_start(k_hl[:, g].bitcast(F32), k_scratch[j, :, g]).then_inc(key_in[g], 16)

            def load_adj(b, j, t, g):
                sp.wait_ge(t_done, 4 * t + g - 3)
                sp.dma_start(adj_s[:, g], adj_t[b, j, g]).then_inc(adj_in[g], 16)

            def load_x(b):
                for c in range(C):
                    sp.dma_start(x_in_s[:, c, 1], xT[b, :, c]).then_inc(x_in[c], 16)

            with sp.Fori(0, NB // 2 - 1) as pair:
                for k in range(2):
                    load_raw(k, keyT[2 * pair + k + 2], 2 * pair + k + 1)
                    store_k(k, 2 * pair + k)
            load_raw(0, valT[0], NB - 1)
            sp.wait_ge(group, 1)
            load_x(0)
            store_k(0, NB - 2)
            sp.wait_ge(k_stored[0], 16)
            for g in range(G):
                load_key(0, g)
            sp.wait_ge(lo_done, NB)
            for g in range(G):
                sp.dma_start(adj_s[:, g], adj_t[0, 0, g]).then_inc(adj_in[g], 16)
            load_raw(0, valT[1], NB + 1)
            store_k(1, NB - 1)
            for k in range(2):
                sp.wait_ge(k_stored[k], 16 * NB // 2)

            def tile(b, j, t, before, block0=False, new_x=None):
                for g in range(G):
                    sp.wait_ge(group, scored(before, g, block0))
                    load_key(j, g)
                    if new_x is None and g:
                        load_adj(b, j, t, g - 1)
                if new_x is None:
                    load_adj(b, j, t, G - 1)
                else:
                    load_x(new_x)
                    for g in range(G):
                        load_adj(b, j, t, g)

            def key_rows(j):
                sp.wait_ge(c_done, j)
                sp.dma_start(y[:], key_t[j]).then_inc(y_in, 16)

            with sp.Fori(1, NB - 1) as j:
                key_rows(j)
                tile(0, j, j, j - 1, block0=True)
                load_raw(0, valT[j + 1], NB + j + 1)
            key_rows(NB - 1)
            tile(0, NB - 1, NB - 1, NB - 2, block0=True)
            tile(1, 0, NB, NB - 1, block0=True, new_x=1)
            sp.wait_ge(c_done, NB)
            sp.dma_start(y[:], x_t[0]).then_inc(y_in, 16)
            tile(1, 1, NB + 1, NB)

            def turn_y(b):
                sp.wait_ge(ln_done, 4 * b + 4)
                sp.dma_start(out_t[b], y[:]).then_inc(out_stored, 16)
                sp.wait_ge(out_stored, 16 * b + 16)

            with sp.Fori(2, NB) as j:
                t = sp.snap(NB + j)
                tile(1, j, t, t - 1)
            with sp.Fori(2, NB) as b:
                t = sp.snap(NB * b)
                tile(b, 0, t, t - 1, new_x=b)
                for j in range(1, 4):
                    tile(b, j, t + j, t + j - 1)
                turn_y(b - 2)
                sp.dma_start(y[:], x_t[b - 1]).then_inc(y_in, 16)
                with sp.Fori(4, NB) as j:
                    tj = sp.snap(NB * b + j)
                    tile(b, j, tj, tj - 1)
            turn_y(NB - 2)
            sp.dma_start(y[:], x_t[NB - 1]).then_inc(y_in, 16)
            for g in range(2):
                sp.wait_ge(ln_done, 4 * (NB - 1) + g + 1)
                sp.dma_start(out_t[NB - 1][:, g], y[:, g]).then_inc(out_stored, 16)
                sp.wait_ge(norm_done, g + 1)
                sp.dma_start(out_t[NB - 1][:, g + 2], y[:, g + 2]).then_inc(out_stored, 16)
            sp.wait_ge(out_stored, 16 * (NB - 1 + G))

        @block.tensor
        def _(pe):
            def times(out, a, b, start, stop, last=True):
                n = len(a)
                for i, ((ah, al), (bh, bl)) in enumerate(zip(a, b)):
                    pe.matmul(out, ah, bh, start=start and i == 0, stop=False, skip_group_check=True)
                    pe.matmul(out, ah, bl, start=False, stop=False, skip_group_check=True)
                    mm = pe.matmul(out, al, bh, start=False, stop=stop and i == n - 1, skip_group_check=True)
                return mm

            pe.wait_ge(wqk_in[0], 32)
            for c in range(C):
                pe.matmul(acc[:, c], wk_s[:, 0, c * P:(c + 1) * P], wq_s[:, 0], start=True, stop=False,
                          skip_group_check=True)
            for o in range(1, C):
                pe.wait_ge(w_split, 2 * o)
                for c in range(C):
                    cols = slice(c * P, (c + 1) * P)
                    mm = times(acc[:, c], [(wk_h[:, o, cols], wk_l[:, o, cols])], [(wq_h[:, o], wq_l[:, o])],
                               False, o == C - 1)
                    if o == C - 1:
                        mm.then_inc(wmm, 1)
            for o in range(C):
                pe.wait_ge(w_split, 2 * C + 2 * o)
                for c in range(C):
                    cols = slice(c * P, (c + 1) * P)
                    mm = times(ps[:, c], [(wv_h[:, o, cols], wv_l[:, o, cols])],
                               [(wm_h[:, o], wm_l[:, o])], o == 0, o == C - 1)
                    if o == C - 1:
                        mm.then_inc(wmm, 1)
                        pe.wait_ge(acc_free, 3)
                        pe.wait_ge(b_in, 80)
                        for i in range(C):
                            mm = pe.matmul(acc[:, 2, c:c + 1], wq_s[:, i, cols], bk_c[:, i:i + 1],
                                           start=i == 0, stop=i == C - 1)
            mm.then_inc(bias_mm, 1)
            pe.wait_ge(reps, 2)
            pe.wait_ge(acc_free, 4)
            for o in range(C):
                mm = pe.matmul(acc[:, 3, 0:1], bq_r[:, o], bk_c[:, o:o + 1], start=o == 0, stop=o == C - 1)
            mm.then_inc(bias_mm, 1)
            for o in range(C):
                mm = pe.matmul(acc[:, 0], bq_r[:, o], wk_s[:, o], start=o == 0, stop=o == C - 1)
            mm.then_inc(wmm, 1)
            for o in range(C):
                pe.matmul(acc[:, 1], bv_r[:, o], wm_s[:, o], start=o == 0, stop=False)
            pe.matmul(acc[:, 1], ones[0:1, :], bm_r[0:1, :], start=False, stop=True).then_inc(wmm, 1)

            def project_key(k, n):
                pe.wait_ge(lo_done, n + 1)
                for e in range(C):
                    pe.wait_ge(acc_free, 4 * n + e + 5)
                    cols = slice(e * P, (e + 1) * P)
                    times(acc[:, e], [(m_h[:, c, cols], m_l[:, c, cols]) for c in range(C)],
                          [(hi[k][:, c], lo[k][:, c]) for c in range(C)], True, True).then_inc(group, 1)

            with pe.Fori(0, NB // 2) as pair:
                for k in range(2):
                    project_key(k, 2 * pair + k)

            def project_value(j):
                for e in range(G):
                    if e == 0:
                        pe.wait_ge(lo_done, NB + j + 1)
                    pe.wait_ge(acc_free, 4 * NB + 4 * j + e + 5)
                    cols = slice(e * P, (e + 1) * P)
                    times(acc[:, e], [(hi[0][:, c, cols], lo[0][:, c, cols]) for c in range(C)],
                          [(wvm_h[:, c], wvm_l[:, c]) for c in range(C)], True, True).then_inc(group, 1)

            def scores(t, g, x_before=None):
                pe.wait_ge(key_in[g], 16 * t + 16)
                pe.wait_ge(s_read, 4 * t + g + 1)
                for c in range(C):
                    if x_before is not None and g == 0:
                        pe.wait_ge(x_lo, x_before + c + 1)
                    mm = times(ps[:, g], [(k_hl[:, g, c, 0], k_hl[:, g, c, 1])],
                               [(x_hl[:, c, 0], x_hl[:, c, 1])], c == 0, c == C - 1)
                mm.then_inc(group, 1)

            def turn_maxima(b):
                pe.wait_ge(mx_done, MX_STEPS * (b + 1))
                for g in range(G):
                    mm = pe.transpose(ps[:, 2, g * P:(g + 1) * P], mx[:, g * P:(g + 1) * P], ident[:])
                mm.then_inc(mx_turned, 1)

            def spread_maxima(b):
                pe.wait_ge(diag_done, b + 1)
                pe.matmul(ps[:, 3], ones[:], diag, start=True, stop=True).then_inc(mx_spread, 1)

            def row_sums(b):
                pe.wait_ge(sum_done, 4 * NB * b + 4 * NB)
                for g in range(G):
                    mm = pe.matmul(ps[:, 2, g:g + 1], p_sums[:, g * P:(g + 1) * P], ones[:, 0:1],
                                   start=True, stop=True)
                mm.then_inc(rowsum_in, 1)

            def product(u, c, first=False, taken=None, squared=None, last=False):
                pe.wait_ge(pl_done, 4 * u + c + 1)
                pe.wait_ge(vl_done, 4 * u + c + 1)
                for g in range(G):
                    if taken is not None and c == 0:
                        pe.wait_ge(acc_read, taken - G + g + 1)
                    if squared is not None and c == 0:
                        pe.wait_ge(sq_done, squared - G + g + 1)
                    rows = slice(g * P, (g + 1) * P)
                    mm = times(acc[:, g], [(p_h[:, c, rows], p_l[:, c, rows])],
                               [(v_h[:, c % 2], v_l[:, c % 2])], first and c == 0, False)
                    if last:
                        mm.then_inc(result, 1)
                if not last:
                    mm.then_inc(pv_done, 1)

            def step(u):
                for g in range(G):
                    scores(u + NB, g)
                for c in range(4):
                    product(u, c)

            def closing_step(u, b, last=False):
                for g in range(G):
                    scores(u + NB, g)
                for c in range(4):
                    product(u, c)
                    if c == (1 if last else 2):
                        turn_maxima(b + 1)
                    if last and c == 2:
                        spread_maxima(b + 1)

            def opening_step(u, b, x_before):
                pe.wait_ge(mx_row_done, b + 1)
                row_sums(b - 1)
                spread_maxima(b)
                scores(u + NB, 0, x_before)
                scores(u + NB, 1)
                pe.wait_ge(rinv_done, b)
                scores(u + NB, 2)
                pe.wait_ge(mx_all_done, b + 1)
                scores(u + NB, 3)
                for c in range(4):
                    product(u, c, first=True, squared=4 * b)

            with pe.Fori(0, NB - 1) as j:
                project_value(j)
                for g in range(G):
                    if g == 0:
                        pe.wait_ge(x_lo, C)
                    scores(j, g)
            for g in range(G):
                scores(NB - 1, g)
            project_value(NB - 1)
            scores(NB, 0, x_before=C)
            turn_maxima(0)
            scores(NB, 1)
            spread_maxima(0)
            pe.wait_ge(mx_all_done, 1)
            scores(NB, 2)
            scores(NB, 3)
            for c in range(4):
                product(0, c, first=True)
            with pe.Fori(0, NB - 2) as b:
                with pe.Fori(1, NB - 1) as j:
                    step(pe.snap(NB * b + j))
                closing_step(pe.snap(NB * b + NB - 1), b)
                opening_step(pe.snap(NB * b + NB), b + 1, 4 * b + 2 * C)
            with pe.Fori(1, NB - 1) as j:
                step(pe.snap(NB * (NB - 2) + j))
            closing_step(NB * (NB - 1) - 1, NB - 2, last=True)
            last = NB * (NB - 1)
            pe.wait_ge(mx_row_done, NB)
            row_sums(NB - 2)
            for c in range(4):
                product(last, c, first=True, taken=4 * (NB - 1))
            pe.wait_ge(rinv_done, NB - 1)
            with pe.Fori(1, NB - 1) as j:
                u = pe.snap(last + j)
                for c in range(4):
                    product(u, c)
            for c in range(3):
                product(last + NB - 1, c)
            row_sums(NB - 1)
            product(last + NB - 1, 3, last=True)

        @block.scalar
        def _(act):
            def split_hi(k, number, loads, groups):
                act.wait_ge(raw_in[k], 16 * loads)
                if groups is not None:
                    act.wait_ge(group, groups)
                act.activation(hi[k][:], raw[k][:], ACT.Copy).then_inc(hi_done, 1)

            for o in range(1, C):
                act.wait_ge(wqk_in[o], 32)
                act.activation(wk_h[:, o], wk_s[:, o], ACT.Copy).then_inc(w_part, 1)
                act.activation(wq_h[:, o], wq_s[:, o], ACT.Copy).then_inc(w_part, 1)
            for o in range(C):
                act.wait_ge(wvm_in[o], 32)
                act.activation(wv_h[:, o], wv_s[:, o], ACT.Copy).then_inc(w_part, 1)
                act.activation(wm_h[:, o], wm_s[:, o], ACT.Copy).then_inc(w_part, 1)
            for c in range(C):
                act.wait_ge(wmm, c + 1)
                act.activation(m_h[:, c], acc[:, c], ACT.Copy, scale=SCALE).then_inc(w_hi, 1)
            split_hi(0, 0, 1, None)
            for c in range(C):
                act.wait_ge(wmm, C + c + 1)
                act.activation(wvm_h[:, c], ps[:, c], ACT.Copy).then_inc(w_hi, 1)

            def k_parts(k, n, stores):
                for c in range(C):
                    act.wait_ge(group, 4 * n + c + 1)
                    if c == 0 and stores is not None:
                        act.wait_ge(k_stored[k], 16 * stores)
                    act.activation(k_out[k][:, :, c, 0], acc[:, c].rearrange("p (g k) -> p g k", k=P),
                                   ACT.Identity, bias=kbias[:, c:c + 1]).then_inc(k_hi, 1)

            act.wait_ge(acc_free, 2 * C)
            split_hi(1, 1, 1, None)
            k_parts(0, 0, None)
            split_hi(0, 2, 2, 4)
            k_parts(1, 1, None)
            with act.Fori(1, NB // 2) as pair:
                for k in range(2):
                    n = 2 * pair + k
                    split_hi(1 - k, n + 1, pair + 1 + k, 4 * n)
                    k_parts(k, n, pair)

            def x_parts(b):
                for c in range(C):
                    act.wait_ge(x_in[c], 16 * b + 16)
                    act.activation(x_hl[:, c, 0], x_in_s[:, c, 1], ACT.Copy).then_inc(x_hi, 1)

            def magnitude(t, g):
                act.wait_ge(s_read, 4 * t + g + 5)
                act.activation(mag[:, g % 2], adj_s[:, g], ACT.Abs).then_inc(mag_done, 1)

            def diagonals(b):
                act.wait_ge(mx_row_done, b + 1)
                for g in range(G):
                    d = act.activation(diag[:, g * P:(g + 1) * P], ident[:], ACT.Copy, scale=mx_row[:, g:g + 1])
                d.then_inc(diag_done, 1)

            def take_maxima(b):
                act.wait_ge(mx_spread, b + 1)
                if not (isinstance(b, int) and b == 0):
                    act.wait_ge(sh_done, 4 * NB * b)
                act.activation(mx_all[:], ps[:, 3], ACT.Copy).then_inc(mx_all_done, 1)

            def v_part(u, j, c):
                if not (isinstance(u, int) and u == 0 and c < 2):
                    act.wait_ge(pv_done, 4 * u + c - 1)
                act.activation(v_h[:, c % 2], v_s[:, 4 * j + c], ACT.Copy).then_inc(vh_done, 1)

            def exp(u, c):
                act.wait_ge(sh_done, 4 * u + c + 1)
                act.activation(prob[:, c], prob[:, c], ACT.Exp).then_inc(exp_done, 1)

            def p_part(u, c):
                act.wait_ge(exp_done, 4 * u + c + 1)
                if not (isinstance(u, int) and u == 0):
                    act.wait_ge(pv_done, 4 * u + c - 3)
                act.activation(p_h[:, c], prob[:, c], ACT.Copy).then_inc(ph_done, 1)

            def squares(b, g, to=acc, ops=None):
                if g == 0 or ops is not None:
                    act.wait_ge(ln_op, LN_OPS * b + 1 if ops is None else ops)
                act.activation(to[:, g], y[:, g], ACT.Square, bias=neg_mean[:, g:g + 1],
                               accum_out=ysq[:, g:g + 1]).then_inc(sq_done, 1)

            def normalised(b, g):
                if g == 0:
                    act.wait_ge(ln_op, LN_OPS * b + LN_OPS)
                act.activation(y[:, g], y[:, g], ACT.Identity, bias=shift[:, g:g + 1],
                               scale=rs[:, g:g + 1]).then_inc(ln_done, 1)

            def step(u, j, first=False, finish=None, leave=None, new_x=None, maxima=None):
                v_part(u, j, 0)
                v_part(u, j, 1)
                if finish is not None:
                    take_maxima(finish + 1)
                    for g in range(G):
                        squares(finish, g)
                exp(u, 0)
                exp(u, 1)
                p_part(u, 0)
                exp(u, 2)
                p_part(u, 1)
                magnitude(u + NB, 0)
                exp(u, 3)
                if leave is not None:
                    normalised(leave, 0)
                magnitude(u + NB, 1)
                p_part(u, 2)
                p_part(u, 3)
                if leave is not None:
                    normalised(leave, 1)
                magnitude(u + NB, 2)
                v_part(u, j, 2)
                if first:
                    v_part(u, j, 3)
                magnitude(u + NB, 3)
                if not first:
                    v_part(u, j, 3)
                if leave is not None:
                    normalised(leave, 2)
                    normalised(leave, 3)
                if new_x is not None:
                    x_parts(new_x)
                if maxima is not None:
                    diagonals(maxima)

            def last_step(u, j, steps=2, before=lambda place: None):
                for c in range(C):
                    for ahead, n in enumerate((c + 1, c + 3, c + 5)):
                        if n // C <= steps:
                            un, jn, cn = u + n // C, j + n // C, n % C
                            if ahead == 0:
                                v_part(un, jn, cn)
                            elif ahead == 1:
                                p_part(un, cn)
                            else:
                                exp(un, cn)
                    before(c)

            def squares_between(place):
                squares(NB - 2, place, x_hl[:, :, 0])

            def normalised_between(place):
                for g in ((), (0,), (1,), (2, 3))[place]:
                    normalised(NB - 2, g)

            x_parts(0)
            with act.Fori(0, NB - 1) as j:
                split_hi(0, None, j + NB // 2 + 2, 4 * NB + 4 + 8 * j)
                for g in range(G):
                    magnitude(j, g)
            magnitude(NB - 1, 0)
            magnitude(NB - 1, 1)
            x_parts(1)
            magnitude(NB - 1, 2)
            magnitude(NB - 1, 3)
            diagonals(0)
            take_maxima(0)
            act.wait_ge(group, 12 * NB)
            step(0, 0, first=True)
            with act.Fori(1, NB - 1) as j:
                step(act.snap(j), j)
            step(NB - 1, NB - 1, new_x=2, maxima=1)

            def turn_over(b, u):
                step(u, 0, first=True, finish=b)
                step(u + 1, 1, leave=b)

            with act.Fori(0, NB - 3) as b:
                u = act.snap(NB * b + NB)
                turn_over(b, u)
                with act.Fori(2, NB - 1) as j:
                    step(act.snap(u + j), j)
                step(act.snap(u + NB - 1), NB - 1, new_x=b + 3, maxima=b + 2)
            turn_over(NB - 3, NB * (NB - 2))
            with act.Fori(2, NB - 1) as j:
                step(act.snap(NB * (NB - 2) + j), j)
            step(NB * (NB - 1) - 1, NB - 1, maxima=NB - 1)
            take_maxima(NB - 1)
            last = NB * (NB - 1)
            v_part(last, 0, 0)
            exp(last, 0)
            exp(last, 1)
            p_part(last, 0)
            exp(last, 2)
            p_part(last, 1)
            exp(last, 3)
            v_part(last, 0, 1)
            p_part(last, 2)
            p_part(last, 3)
            v_part(last, 0, 2)
            squares_between(0)
            exp(last + 1, 0)
            exp(last + 1, 1)
            p_part(last + 1, 0)
            v_part(last, 0, 3)
            squares_between(1)
            exp(last + 1, 2)
            p_part(last + 1, 1)
            v_part(last + 1, 1, 0)
            squares_between(2)
            exp(last + 1, 3)
            p_part(last + 1, 2)
            squares_between(3)
            exp(last + 2, 0)
            last_step(last + 1, 1, before=normalised_between)
            with act.Fori(2, NB - 2) as j:
                last_step(act.snap(last + j), j)
            last_step(last + NB - 2, NB - 2, steps=1)
            last_step(last + NB - 1, NB - 1, steps=0)
            for g in range(G):
                squares(NB - 1, g, x_hl[:, :, 1], ops=LN_OPS * (NB - 1) + g + 1)
            act.wait_ge(ln_op, LN_OPS * NB + G - 1)
            for g in range(2):
                act.activation(y[:, g], y[:, g], ACT.Identity, bias=shift[:, g:g + 1],
                               scale=rs[:, g:g + 1]).then_inc(ln_done, 1)

        @block.vector
        def _(dve):
            def minus_hi(lo_part, whole, hi_part):
                return dve.tensor_tensor(lo_part, whole, hi_part.bitcast(F32), ALU.subtract)

            def split_lo(k, number):
                dve.wait_ge(hi_done, number + 1)
                minus_hi(lo[k][:], raw[k][:], hi[k][:]).then_inc(lo_done, 1)

            dve.memset(ones[:], 1.0).then_inc(reps, 1)
            for o in range(1, C):
                for i, (w, high, low) in enumerate(((wk_s, wk_h, wk_l), (wq_s, wq_h, wq_l))):
                    dve.wait_ge(w_part, 2 * o - 1 + i)
                    minus_hi(low[:, o], w[:, o], high[:, o]).then_inc(w_split, 1)
            dve.wait_ge(b_in, 80)
            dve.wait_ge(reps, 1)
            for o in range(C):
                dve.tensor_scalar(bq_r[:, o], ones[:], bq_c[:, o:o + 1], None, ALU.mult)
                last = dve.tensor_scalar(bv_r[:, o], ones[:], bv_c[:, o:o + 1], None, ALU.mult)
            last.then_inc(reps, 1)
            for o in range(C):
                for i, (w, high, low) in enumerate(((wv_s, wv_h, wv_l), (wm_s, wm_h, wm_l))):
                    dve.wait_ge(w_part, 2 * (C - 1) + 2 * o + 1 + i)
                    minus_hi(low[:, o], w[:, o], high[:, o]).then_inc(w_split, 1)
            for c in range(C):
                dve.wait_ge(w_hi, c + 1)
                dve.scalar_tensor_tensor(m_l[:, c], acc[:, c], SCALE, m_h[:, c].bitcast(F32),
                                         ALU.mult, ALU.subtract).then_inc(acc_free, 1)
            split_lo(0, 0)
            for c in range(C):
                dve.wait_ge(w_hi, C + c + 1)
                minus_hi(wvm_l[:, c], ps[:, c], wvm_h[:, c]).then_inc(s_read, 1)
            dve.wait_ge(wmm, 2 * C + 1)
            dve.tensor_scalar(w1[:], acc[:, 0], SCALE, None, ALU.mult).then_inc(acc_free, 1)
            dve.wait_ge(wmm, 2 * C + 2)
            dve.tensor_copy(vbias[:], acc[:, 1]).then_inc(acc_free, 1)
            dve.wait_ge(bias_mm, 1)
            dve.tensor_scalar(kbias[:], acc[:, 2, 0:C], SCALE, None, ALU.mult).then_inc(acc_free, 1)
            dve.wait_ge(bias_mm, 2)
            dve.tensor_scalar(rbias[:], acc[:, 3, 0:1], SCALE, None, ALU.mult).then_inc(acc_free, 1)
            dve.wait_ge(acc_free, 2 * C)

            def k_parts(k, n):
                for c in range(C):
                    dve.wait_ge(k_hi, 4 * n + c + 1)
                    dve.scalar_tensor_tensor(k_out[k][:, :, c, 1], acc[:, c].rearrange("p (g k) -> p g k", k=P),
                                             kbias[:, c:c + 1], k_out[k][:, :, c, 0].bitcast(F32), ALU.add,
                                             ALU.subtract).then_inc(acc_free, 1)

            with dve.Fori(0, NB // 2) as pair:
                for k in range(2):
                    split_lo(1 - k, 2 * pair + k + 1)
                    k_parts(k, 2 * pair + k)

            def own_terms(j):
                dve.wait_ge(y_in, 16 * j + 16)
                for c in range(C):
                    dve.tensor_tensor_reduce(y[:, c], y[:, c], w1[:], 1.0, 0.0, ALU.mult, ALU.add,
                                             c_new[:, c:c + 1]).then_inc(c_part, 1)
                dve.wait_ge(c_part, 4 * j + 4)
                dve.tensor_scalar(c_all[:, bass.ds(4 * j, G)], c_new[:], rbias[:, 0:1], None,
                                  ALU.add).then_inc(c_done, 1)

            def v_tile(j):
                for c in range(G):
                    last = isinstance(j, int) and j == NB - 1
                    dve.wait_ge(group, 12 * NB if last else valued(j, c))
                    dve.tensor_tensor(v_s[:, bass.ds(4 * j + c, 1)], acc[:, c], vbias[:], ALU.add).then_inc(acc_free, 1)

            def weighted(j, t, g, groups):
                dve.wait_ge(group, groups)
                dve.wait_ge(adj_in[g], 16 * t + 16)
                dve.scalar_tensor_tensor(adj_s[:, g], ps[:, g], c_all[:, bass.ds(4 * j + g, 1)],
                                         adj_s[:, g], ALU.add, ALU.mult).then_inc(s_read, 1)

            def masked(j, t, g):
                dve.wait_ge(mag_done, 4 * t + g + 1)
                dve.tensor_scalar(cut[:], mag[:, g % 2], CUT, None, ALU.is_lt).then_inc(cut_done, 1)
                dve.wait_ge(cut_done, 4 * t + g + 1)
                dve.scalar_tensor_tensor(t_s[:, g, j], cut[:], MASKED, adj_s[:, g],
                                         ALU.mult, ALU.add).then_inc(t_done, 1)

            def maximum(j, t, g, first):
                if first and g == 0:
                    return
                dve.wait_ge(t_done, 4 * t + g + 1)
                dve.tensor_tensor(mx[:], t_s[:, 0, j] if first and g == 1 else mx[:], t_s[:, g, j],
                                  ALU.max).then_inc(mx_done, 1)

            def row_maxima(b):
                dve.wait_ge(mx_turned, b + 1)
                dve.tensor_reduce(mx_row[:], ps[:, 2].rearrange("p (g k) -> p g k", k=P), AX.X,
                                  ALU.max).then_inc(mx_row_done, 1)
            def shifted(u, j, c):
                dve.tensor_tensor(prob[:, c], t_s[:, c, j], mx_all[:], ALU.subtract).then_inc(sh_done, 1)

            def x_parts(b):
                for c in range(C):
                    dve.wait_ge(x_hi, 4 * b + c + 1)
                    minus_hi(x_hl[:, c, 1], x_in_s[:, c, 1], x_hl[:, c, 0]).then_inc(x_lo, 1)

            def v_part(u, j, c):
                dve.wait_ge(vh_done, 4 * u + c + 1)
                minus_hi(v_l[:, c % 2], v_s[:, 4 * j + c], v_h[:, c % 2]).then_inc(vl_done, 1)

            def p_part(u, c):
                dve.wait_ge(ph_done, 4 * u + c + 1)
                minus_hi(p_l[:, c], prob[:, c], p_h[:, c]).then_inc(pl_done, 1)

            def add_up(u, c, first):
                if first and c == 0:
                    dve.tensor_copy(p_sums[:], prob[:, c]).then_inc(sum_done, 1)
                else:
                    dve.wait_ge(sum_done, 4 * u + c)
                    dve.tensor_tensor(p_sums[:], p_sums[:], prob[:, c], ALU.add).then_inc(sum_done, 1)

            def invert_sums(b):
                dve.wait_ge(rowsum_in, b + 1)
                dve.reciprocal(rinv[:], ps[:, 2, 0:G]).then_inc(rinv_done, 1)

            def take_out(b, g, last=False):
                if g == 0:
                    dve.wait_ge(rinv_done, b + 1)
                    dve.wait_ge(y_in, 16 * (NB + b + 1))
                    if not last:
                        dve.wait_ge(pv_done, 4 * NB * b + 4 * NB)
                if last:
                    dve.wait_ge(result, g + 1)
                dve.scalar_tensor_tensor(y[:, g], acc[:, g], rinv[:, g:g + 1], y[:, g], ALU.mult, ALU.add,
                                         accum_out=ysum[:, g:g + 1]).then_inc(acc_read, 1)

            def ln_step(b, n, more=0):
                if n == 1:
                    dve.wait_ge(acc_read, 4 * b + 4)
                    step_n = dve.tensor_scalar(neg_mean[:], ysum[:], -1.0 / D, None, ALU.mult)
                elif n == 2:
                    dve.wait_ge(sq_done, 4 * b + 4)
                    step_n = dve.tensor_scalar(ve[:], ysq[:], 1.0 / D, EPS, ALU.mult, ALU.add)
                else:
                    dve.wait_ge(ln_op, LN_OPS * b + n - 1 + more)
                    if n == 3:
                        step_n = dve.tensor_scalar(nt[:].bitcast(I32), ve[:].bitcast(I32), 1, None,
                                                   ALU.arith_shift_right)
                    elif n == 4:
                        step_n = dve.tensor_scalar(rs[:].bitcast(I32), nt[:].bitcast(I32), -1.0,
                                                   float(0x5f3759df), ALU.mult, ALU.add)
                    elif n == LN_OPS:
                        step_n = dve.tensor_tensor(shift[:], neg_mean[:], rs[:], ALU.mult)
                    elif n % 3 == 2:
                        step_n = dve.scalar_tensor_tensor(nt[:], rs[:], -0.5, rs[:], ALU.mult, ALU.mult)
                    elif n % 3 == 0:
                        step_n = dve.tensor_tensor(nt[:], nt[:], ve[:], ALU.mult)
                    else:
                        step_n = dve.scalar_tensor_tensor(rs[:], nt[:], 1.5, rs[:], ALU.add, ALU.mult)
                step_n.then_inc(ln_op, 1)

            def ln_steps(b, steps):
                if b is not None:
                    for n in steps:
                        ln_step(b, n)

            def step(u, j, b=None, first=False, closing=None, new_x=True):
                t = u + NB
                if b is not None:
                    invert_sums(b)
                    for g in range(G):
                        take_out(b, g)
                    ln_step(b, 1)
                if first:
                    dve.wait_ge(mx_all_done, 1 if b is None else b + 2)
                shifted(u, j, 0)
                shifted(u, j, 1)
                v_part(u, j, 0)
                v_part(u, j, 1)
                shifted(u, j, 2)
                if not (isinstance(u, int) and u == 0):
                    dve.wait_ge(sum_done, 4 * u)
                shifted(u, j, 3)
                weighted(j, t, 0, scored(t, 0))
                p_part(u, 0)
                p_part(u, 1)
                masked(j, t, 0)
                weighted(j, t, 1, scored(t, 1))
                ln_steps(b, (2,))
                maximum(j, t, 0, first)
                ln_steps(b, (3,))
                masked(j, t, 1)
                ln_steps(b, (4,))
                add_up(u, 0, first)
                weighted(j, t, 2, scored(t, 2))
                ln_steps(b, (5,))
                p_part(u, 2)
                if first:
                    v_part(u, j, 2)
                p_part(u, 3)
                ln_steps(b, (6,))
                maximum(j, t, 1, first)
                masked(j, t, 2)
                if not first:
                    v_part(u, j, 2)
                ln_steps(b, (7,))
                weighted(j, t, 3, scored(t, 3))
                ln_steps(b, (8,))
                if first:
                    v_part(u, j, 3)
                maximum(j, t, 2, first)
                masked(j, t, 3)
                ln_steps(b, (9,))
                if closing is not None:
                    maximum(j, t, 3, first)
                if not first:
                    v_part(u, j, 3)
                add_up(u, 1, first)
                ln_steps(b, (10,))
                if closing is None:
                    maximum(j, t, 3, first)
                ln_steps(b, (11,))
                add_up(u, 2, first)
                ln_steps(b, (12,))
                add_up(u, 3, first)
                if closing is not None:
                    row_maxima(closing)
                    if new_x:
                        x_parts(closing + 1)
                ln_steps(b, (13, 14))

            def last_step(u, j, steps=2, finish=()):
                for c in range(C):
                    for ahead, n in enumerate((c + 1, c + 3, c + 6)):
                        if n // C <= steps:
                            un, jn, cn = u + n // C, j + n // C, n % C
                            if ahead == 0:
                                v_part(un, jn, cn)
                            elif ahead == 1:
                                p_part(un, cn)
                                add_up(un, cn, False)
                            else:
                                dve.wait_ge(sum_done, 4 * (un - 1) + cn + 1)
                                shifted(un, jn, cn)
                    if finish and c < 2:
                        ln_steps(NB - 2, finish[c])

            def first_scores(j, first=False, last=False):
                for g in range(G):
                    weighted(j, j, g, scored(j, g, block0=True))
                    if last and g == 2:
                        x_parts(1)
                    if g:
                        maximum(j, j, g - 1, first)
                    masked(j, j, g)
                maximum(j, j, G - 1, first)

            def first_tiles(j, first=False):
                own_terms(j)
                if first:
                    x_parts(0)
                v_tile(j)
                split_lo(0, NB + 1 + j)
                dve.wait_ge(c_done, j + 1)
                first_scores(j, first)

            first_tiles(0, first=True)
            with dve.Fori(1, NB - 1) as j:
                first_tiles(j)
            own_terms(NB - 1)
            dve.wait_ge(c_done, NB)
            first_scores(NB - 1, last=True)
            v_tile(NB - 1)
            row_maxima(0)
            step(0, 0, first=True)
            with dve.Fori(0, NB - 2) as b:
                with dve.Fori(1, NB - 1) as j:
                    step(dve.snap(NB * b + j), j)
                step(dve.snap(NB * b + NB - 1), NB - 1, closing=b + 1)
                step(dve.snap(NB * b + NB), 0, b=b, first=True)
            with dve.Fori(1, NB - 1) as j:
                step(dve.snap(NB * (NB - 2) + j), j)
            step(NB * (NB - 1) - 1, NB - 1, closing=NB - 1, new_x=False)
            last = NB * (NB - 1)
            dve.wait_ge(mx_all_done, NB)
            shifted(last, 0, 0)
            shifted(last, 0, 1)
            v_part(last, 0, 0)
            shifted(last, 0, 2)
            dve.wait_ge(sum_done, 4 * last)
            shifted(last, 0, 3)
            p_part(last, 0)
            invert_sums(NB - 2)
            for g in range(G):
                take_out(NB - 2, g)
            p_part(last, 1)
            v_part(last, 0, 1)
            ln_step(NB - 2, 1)
            p_part(last, 2)
            add_up(last, 0, True)
            add_up(last, 1, False)

            def shifted_next(n):
                dve.wait_ge(sum_done, 4 * last + n - 3)
                shifted(last + n // C, n // C, n % C)

            v_part(last, 0, 2)
            shifted_next(4)
            add_up(last, 2, False)
            shifted_next(5)
            p_part(last, 3)
            add_up(last, 3, False)
            shifted_next(6)
            v_part(last, 0, 3)
            p_part(last + 1, 0)
            add_up(last + 1, 0, False)
            shifted_next(7)
            v_part(last + 1, 1, 0)
            p_part(last + 1, 1)
            add_up(last + 1, 1, False)
            shifted_next(8)
            p_part(last + 1, 2)
            add_up(last + 1, 2, False)
            shifted_next(9)
            last_step(last + 1, 1, finish=(range(2, 8), range(8, LN_OPS + 1)))
            with dve.Fori(2, NB - 2) as j:
                last_step(dve.snap(last + j), j)
            last_step(last + NB - 2, NB - 2, steps=1)
            last_step(last + NB - 1, NB - 1, steps=0)
            invert_sums(NB - 1)
            for g in range(G):
                take_out(NB - 1, g, last=True)
                dve.wait_ge(acc_read, 4 * (NB - 1) + g + 1)
                dve.tensor_scalar(neg_mean[:, g:g + 1], ysum[:, g:g + 1], -1.0 / D, None, ALU.mult).then_inc(ln_op, 1)
            for n in range(2, LN_OPS + 1):
                ln_step(NB - 1, n, more=G - 1)
            dve.wait_ge(ln_op, LN_OPS * NB + G - 1)
            for g in range(2, G):
                dve.tensor_scalar(y[:, g], y[:, g], rs[:, g:g + 1], shift[:, g:g + 1], ALU.mult,
                                  ALU.add).then_inc(norm_done, 1)


def kernel(x, adj, L0_gnn_key, L0_gnn_value, L0_gnn_Wq, L0_gnn_bq, L0_gnn_Wk, L0_gnn_bk,
           L0_gnn_Wv, L0_gnn_bv, L0_gnn_Wm, L0_gnn_bm):
    import numpy as _np
    import concourse.bacc as _bacc
    from concourse.bass_utils import run_bass_kernel_spmd as _run

    def tiles(a):
        a = _np.asarray(a).reshape(NB, W, C, P)
        return _np.ascontiguousarray(a.transpose(0, 3, 2, 1))

    def column(a):
        return _np.ascontiguousarray(_np.asarray(a).reshape(C, P).T)

    arrays = {
        "x": _np.ascontiguousarray(x), "adjT": _np.ascontiguousarray(_np.asarray(adj).T),
        "xT": tiles(x), "key": _np.ascontiguousarray(L0_gnn_key),
        "keyT": tiles(L0_gnn_key), "valT": tiles(L0_gnn_value),
        "Wq": _np.ascontiguousarray(L0_gnn_Wq), "Wk": _np.ascontiguousarray(L0_gnn_Wk),
        "Wv": _np.ascontiguousarray(L0_gnn_Wv), "WmT": _np.ascontiguousarray(_np.asarray(L0_gnn_Wm).T),
        "bq": column(L0_gnn_bq), "bk": column(L0_gnn_bk), "bv": column(L0_gnn_bv),
        "bm": _np.ascontiguousarray(_np.asarray(L0_gnn_bm).reshape(1, D)),
        "ident": _np.eye(P, dtype=_np.float32),
    }
    nc = _bacc.Bacc("TRN2", target_bir_lowering=False, num_devices=1, dynamic_dma_scratch_size=1024)
    args = [nc.dram_tensor(f"in_{n}_dram", a.shape, F32, kind="ExternalInput").ap() for n, a in arrays.items()]
    k_scratch = nc.dram_tensor("k_scratch", (NB, P, G, C, 2, P), F32, kind="Internal").ap()
    out = nc.dram_tensor("out_dram", (N, D), F32, kind="ExternalOutput").ap()
    gnn_attention_kernel(nc, *args, k_scratch, out)
    r = _run(nc, [{f"in_{n}_dram": a for n, a in arrays.items()}], core_ids=[0])
    return r.results[0]["out_dram"]
```
